# Optimizing a Trainium2 kernel written in Bass

```python
import numpy as np
import jax
import jax.numpy as jnp

def _softmax(x, axis=-1):
    return jax.nn.softmax(x, axis=axis)

def _gelu(x):
    return jax.nn.gelu(x, approximate=True)

def _silu(x):
    return jax.nn.silu(x)

def _sigmoid(x):
    return jax.nn.sigmoid(x)

def _layernorm(x, axis=-1, eps=1e-05):
    m = jnp.mean(x, axis=axis, keepdims=True)
    v = jnp.var(x, axis=axis, keepdims=True)
    return (x - m) / jnp.sqrt(v + eps)

def _scatter_add(tgt, idx, src, axis=0):
    return tgt.at[idx].add(src)

def _segment_sum(src, seg, n):
    return jax.ops.segment_sum(src, seg, n)
kernel_name = 'mk_adaln_ffn_d1_seqx_r4_35b4e8'

def setup_inputs(seed: int=0):
    np.random.seed(seed)
    _w = jnp.asarray

    def _rec_inputs():
        import jax
        import jax.numpy as jnp
        _rk = jax.random.key(seed)
        x = -0.000125 + 0.9999 * jax.random.normal(jax.random.fold_in(_rk, 1), (128, 64, 1024), jnp.float32)
        _lenS = 64 - jax.random.randint(jax.random.fold_in(_rk, 7), (128,), 0, max(1, 64 // 4) + 1, jnp.int32)
        _lenS2 = 64 - jax.random.randint(jax.random.fold_in(_rk, 8), (128,), 0, max(1, 64 // 4) + 1, jnp.int32)
        cond_128 = 0.0061147 + 1.02565 * jax.random.normal(jax.random.fold_in(_rk, 11), (128, 128), jnp.float32)
        return (x, cond_128)
    x, cond_128 = _rec_inputs()

    def _L0_cond_setup():
        import jax, jax.numpy as jnp
        import numpy as np
        K = 8
        T = 1.0
        D_EMBD = 128
        IN_C = 64
        OUT_C = 64
        BS = 32
        H = 1024
        HID = 128
        key = jax.random.key(seed)
        ks = jax.random.split(key, 10)
        s = lambda fan_in: 1.0 / np.sqrt(fan_in)
        return {'x': jax.random.normal(ks[0], (BS, IN_C, H), dtype=jnp.float32), 'embedding': jax.random.normal(ks[1], (BS, D_EMBD), dtype=jnp.float32), 'W0': jax.random.normal(ks[2], (D_EMBD, HID), dtype=jnp.float32) * s(D_EMBD), 'b0': jnp.zeros((HID,), dtype=jnp.float32), 'W1': jax.random.normal(ks[3], (HID, HID), dtype=jnp.float32) * s(HID), 'b1': jnp.zeros((HID,), dtype=jnp.float32), 'W2': jax.random.normal(ks[4], (HID, K), dtype=jnp.float32) * s(HID), 'b2': jnp.zeros((K,), dtype=jnp.float32), 'weight': jax.random.normal(ks[5], (K, OUT_C, IN_C, 1), dtype=jnp.float32) * s(IN_C), 'bias_k': jax.random.normal(ks[6], (K, OUT_C), dtype=jnp.float32) * 0.1}
    _L0_cond_all = _L0_cond_setup()
    _L0_cond_in = {k: v for k, v in _L0_cond_all.items() if k in ('W0', 'b0', 'W1', 'b1', 'W2', 'b2', 'weight', 'bias_k')}
    del _L0_cond_all

    def _L0_ffn_setup():
        import jax, jax.numpy as jnp
        import numpy as np
        R = 16
        NUM_EXPERTS = 8
        TOP_K = 2
        LORA_ALPHA = 32
        SCALING = LORA_ALPHA / R
        key = jax.random.key(seed)
        ks = jax.random.split(key, 6)
        d_in, d_out = (1024, 1024)
        x = jax.random.normal(ks[0], (4, 512, d_in), dtype=jnp.float32)
        W_base = jax.random.normal(ks[1], (d_out, d_in), dtype=jnp.float32) * 0.02
        b_base = jax.random.normal(ks[2], (d_out,), dtype=jnp.float32) * 0.02
        W_router = jax.random.normal(ks[3], (NUM_EXPERTS, d_in), dtype=jnp.float32) * 0.01
        A = jax.random.normal(ks[4], (NUM_EXPERTS, R, d_in), dtype=jnp.float32) * 0.02
        B = jax.random.normal(ks[5], (NUM_EXPERTS, d_out, R), dtype=jnp.float32) * 0.02
        return {'x': x, 'W_base': W_base, 'b_base': b_base, 'W_router': W_router, 'A': A, 'B': B}
    _L0_ffn_all = _L0_ffn_setup()
    _L0_ffn_in = {k: v for k, v in _L0_ffn_all.items() if k in ('W_base', 'b_base', 'W_router', 'A', 'B')}
    del _L0_ffn_all
    return {'x': x, 'cond_128': cond_128, 'L0_cond_W0': _L0_cond_in['W0'], 'L0_cond_b0': _L0_cond_in['b0'], 'L0_cond_W1': _L0_cond_in['W1'], 'L0_cond_b1': _L0_cond_in['b1'], 'L0_cond_W2': _L0_cond_in['W2'], 'L0_cond_b2': _L0_cond_in['b2'], 'L0_cond_weight': _L0_cond_in['weight'], 'L0_cond_bias_k': _L0_cond_in['bias_k'], 'L0_ffn_W_base': _L0_ffn_in['W_base'], 'L0_ffn_b_base': _L0_ffn_in['b_base'], 'L0_ffn_W_router': _L0_ffn_in['W_router'], 'L0_ffn_A': _L0_ffn_in['A'], 'L0_ffn_B': _L0_ffn_in['B']}

def reference(x, cond_128, L0_cond_W0, L0_cond_b0, L0_cond_W1, L0_cond_b1, L0_cond_W2, L0_cond_b2, L0_cond_weight, L0_cond_bias_k, L0_ffn_W_base, L0_ffn_b_base, L0_ffn_W_router, L0_ffn_A, L0_ffn_B):
    import jax
    import jax.numpy as jnp

    def _L0_cond_ref(x, embedding, W0, b0, W1, b1, W2, b2, weight, bias_k):
        import jax, jax.numpy as jnp
        import numpy as np
        K = 8
        T = 1.0
        D_EMBD = 128
        IN_C = 64
        OUT_C = 64
        BS = 32
        H = 1024
        HID = 128
        h = jax.nn.gelu(embedding @ W0 + b0, approximate=False)
        h = jax.nn.gelu(h @ W1 + b1, approximate=False)
        att = jax.nn.softmax((h @ W2 + b2) / T, axis=-1)
        agg_w = jnp.einsum('bk,koi->boi', att, weight[..., 0])
        agg_b = att @ bias_k
        out = jnp.einsum('boi,bih->boh', agg_w, x) + agg_b[:, :, None]
        return out

    def _L0_ffn_ref(x, W_base, b_base, W_router, A, B):
        import jax, jax.numpy as jnp
        import numpy as np
        R = 16
        NUM_EXPERTS = 8
        TOP_K = 2
        LORA_ALPHA = 32
        SCALING = LORA_ALPHA / R
        orig_shape = x.shape
        d_in = x.shape[-1]
        x_flat = x.reshape(-1, d_in)
        logits = x_flat @ W_router.T
        probs = jax.nn.softmax(logits, axis=-1)
        topk_probs, topk_idx = jax.lax.top_k(probs, TOP_K)
        topk_probs = topk_probs / jnp.sum(topk_probs, axis=-1, keepdims=True)
        onehot = jax.nn.one_hot(topk_idx, NUM_EXPERTS, dtype=x.dtype)
        combine = jnp.einsum('nk,nke->ne', topk_probs, onehot)
        h = jnp.einsum('nd,erd->ner', x_flat, A)
        hw = h * combine[:, :, None]
        expert_out = jnp.einsum('ner,eor->no', hw, B) * SCALING
        base_out = x_flat @ W_base.T + b_base
        out = base_out + expert_out
        return out.reshape(*orig_shape[:-1], W_base.shape[0])
    x = x + _L0_ffn_ref(_L0_cond_ref(x, cond_128, L0_cond_W0, L0_cond_b0, L0_cond_W1, L0_cond_b1, L0_cond_W2, L0_cond_b2, L0_cond_weight, L0_cond_bias_k), L0_ffn_W_base, L0_ffn_b_base, L0_ffn_W_router, L0_ffn_A, L0_ffn_B)
    return x

_drawn_inputs = setup_inputs


def setup_inputs(seed=0):
    import zlib

    import numpy as np

    out = dict(_drawn_inputs(seed))
    spreads = {'L0_cond_b0': (0.0, 0.778), 'L0_cond_b1': (0.0, 0.466), 'L0_cond_b2': (0.0, 0.446)}
    factors = {'L0_ffn_b_base': 2.874}
    for name, (base, spread) in spreads.items():
        noise = np.random.default_rng([zlib.crc32(name.encode()), seed]).standard_normal(out[name].shape)
        drawn = base * np.exp(spread * noise) if base else spread * noise
        out[name] = jnp.asarray(drawn.astype(out[name].dtype))
    for name, factor in factors.items():
        out[name] = (out[name] * factor).astype(out[name].dtype)
    return out
```

```python
from contextlib import ExitStack

import numpy as np

import concourse.bass as bass
from concourse import mybir

ALU = mybir.AluOpType
ACT = mybir.ActivationFunctionType
F32 = mybir.dt.float32
F32R = mybir.dt.float32r
U32 = mybir.dt.uint32
AX_X = mybir.AxisListType.X

P = 128
BATCH, CH, D = 128, 64, 1024
HID = 128
KERNELS = 8
EXPERTS, RANK = 8, 16
ER = EXPERTS * RANK
PAIR = P // CH
TILES = BATCH // PAIR
DC = D // P
HALF = 512
AR = ER + EXPERTS
SLOTS = 4
STAGE = 4
O_BANK = HALF // TILES
LORA_SCALE = 2.0

C_IDENT, C_PAIR, C_PARITY, C_IOTA, C_DIAG, C_END = 0, 128, 192, 208, 224, 352


def shape_constants():
    c = np.zeros((P, C_END), np.float32)
    b = np.arange(P)
    c[b, C_IDENT + b] = 1.0
    c[b, C_PAIR + b // PAIR] = 1.0
    for par in range(PAIR):
        c[b % PAIR == par, C_PARITY + par * KERNELS:C_PARITY + (par + 1) * KERNELS] = 1.0
    c[:, C_IOTA:C_IOTA + EXPERTS] = np.arange(EXPERTS)
    c[:, C_IOTA + EXPERTS:C_DIAG] = np.arange(EXPERTS)
    for s in range(PAIR):
        c[s * CH:(s + 1) * CH, C_DIAG + s * CH:C_DIAG + (s + 1) * CH] = 1.0
    return c


def build(nc, x, condT, w0, b0, w1, b1, w2, b2, mix_w, mix_b, wT, b_base, arT, bT, consts, out):
    x_tiles = x.rearrange("(t p) h -> t p h", p=P)
    out_tiles = out.rearrange("(t p) h -> t p h", p=P)
    wT_chunks = wT.rearrange("(c p) n -> c p n", p=P)
    agg_b_dram = nc.dram_tensor("agg_b_rows", (BATCH, CH), F32, kind="Internal").ap()

    with ExitStack() as ctx:
        def sb(name, shape, dt=F32):
            return ctx.enter_context(nc.sbuf_tensor(name, shape, dt))

        def sem(name):
            return ctx.enter_context(nc.semaphore(name))

        w_hi = sb("w_hi", [P, DC, D], F32R)
        w_lo = sb("w_lo", [P, DC, D], F32R)
        ar_hi = sb("ar_hi", [P, DC, AR], F32R)
        ar_lo = sb("ar_lo", [P, DC, AR], F32R)
        b_hi = sb("b_hi", [P, D], F32R)
        b_lo = sb("b_lo", [P, D], F32R)
        agg_w = sb("agg_w", [P, TILES, CH])
        agg_b = sb("agg_b", [P, TILES * P])
        bias_out = sb("bias_out", [P, D])
        x_sb = sb("x_sb", [P, SLOTS, D])
        x_hi = sb("x_hi", [P, D], F32R)
        x_lo = sb("x_lo", [P, D], F32R)
        mix_hi = sb("mix_hi", [P, P], F32R)
        mix_lo = sb("mix_lo", [P, P], F32R)
        mix_pair = sb("mix_pair", [P, CH])
        mix_f32 = sb("mix_f32", [P, P])
        y_sb = sb("y_sb", [P, D])
        y_hi = sb("y_hi", [P, 2, D], F32R)
        y_lo = sb("y_lo", [P, 2, D], F32R)
        top_val = sb("top_val", [P, 8])
        logits_sb = sb("logits_sb", [P, EXPERTS])
        top_gap = sb("top_gap", [P, 1])
        top_idx = sb("top_idx", [P, 8], U32)
        picked = sb("picked", [P, 2, EXPERTS])
        ratio = sb("ratio", [P, 1])
        half_sum = sb("half_sum", [P, 1])
        first_w = sb("first_w", [P, 1])
        expert_w = sb("expert_w", [P, EXPERTS])
        hw = sb("hw", [P, ER])
        hwT_hi = sb("hwT_hi", [P, P], F32R)
        hwT_lo = sb("hwT_lo", [P, P], F32R)
        w_stage = sb("w_stage", [P, STAGE, DC * AR])
        mixw = agg_b[0:PAIR * KERNELS, :].rearrange("p (o n) -> p o n", o=CH)
        consts_sb = sb("consts_sb", [P, C_END])
        condT_sb = sb("condT_sb", [P, BATCH])
        w0_sb = sb("w0_sb", [P, HID])
        w1_sb = sb("w1_sb", [P, HID])
        w2_sb = sb("w2_sb", [P, KERNELS])
        b0_sb = sb("b0_sb", [P, 1])
        b1_sb = sb("b1_sb", [P, 1])
        b2_sb = sb("b2_sb", [P, KERNELS])
        mix_b_sb = sb("mix_b_sb", [KERNELS, CH])
        h1T = sb("h1T", [P, BATCH])
        h2T = sb("h2T", [P, BATCH])
        score = sb("score", [P, KERNELS])
        neg_max = sb("neg_max", [P, 1])
        score_exp = sb("score_exp", [P, KERNELS])
        exp_sum = sb("exp_sum", [P, 1])
        exp_inv = sb("exp_inv", [P, 1])
        att = sb("att", [P, KERNELS])
        att_par = sb("att_par", [P, PAIR * KERNELS])
        attT = sb("attT", [KERNELS, BATCH])
        attT_par = sb("attT_par", [PAIR * KERNELS, TILES])
        agg_b_rows = sb("agg_b_rows_sb", [P, CH])

        ident = consts_sb[:, C_IDENT:C_IDENT + P]
        pair_sel = consts_sb[:, C_PAIR:C_PAIR + TILES]
        parity = consts_sb[:, C_PARITY:C_PARITY + PAIR * KERNELS]
        diagonal = consts_sb[:, C_DIAG:C_END].rearrange("p (s o) -> p s o", s=PAIR)
        expert_no = consts_sb[:, C_IOTA:C_DIAG].rearrange("p (s e) -> p s e", s=2)

        ps_out = ctx.enter_context(nc.psum_tensor("ps_out", [P, 2, D], F32))
        ps_y = ctx.enter_context(nc.psum_tensor("ps_y", [P, D], F32))
        ps_ar = ctx.enter_context(nc.psum_tensor("ps_ar", [P, HALF], F32))
        ps_hwT = ctx.enter_context(nc.psum_tensor("ps_hwT", [P, HALF], F32))
        ps_agg = [ps_out[:, g // 2, g % 2 * HALF:(g % 2 + 1) * HALF] for g in range(4)]

        consts_in = sem("consts_in")
        cond_in = sem("cond_in")
        mixw_in = sem("mixw_in")
        w_in = [sem(f"w_in{s}") for s in range(STAGE)]
        bias_out_in = sem("bias_out_in")
        cond_mm = sem("cond_mm")
        gelu_done = sem("gelu_done")
        att_step = sem("att_step")
        score_exped = sem("score_exped")
        agg_mm = sem("agg_mm")
        agg_done = sem("agg_done")
        agg_b_out = sem("agg_b_out")
        agg_b_in = [sem("agg_b_in_first"), sem("agg_b_in_rest")]
        w_hi_done = sem("w_hi_done")
        w_lo_done = sem("w_lo_done")
        x_in = [sem(f"x_in{s}") for s in range(SLOTS)]
        stored = [sem(f"stored{s}") for s in range(SLOTS)]
        x_hi_done = sem("x_hi_done")
        x_lo_done = sem("x_lo_done")
        x_biased = sem("x_biased")
        mix_step = sem("mix_step")
        mix_done = sem("mix_done")
        y_mm = sem("y_mm")
        y_summed = sem("y_summed")
        y_hi_done = sem("y_hi_done")
        y_lo_done = sem("y_lo_done")
        ar_mm = sem("ar_mm")
        ratio_done = sem("ratio_done")
        routed = sem("routed")
        hw_done = sem("hw_done")
        hwT_mm = sem("hwT_mm")
        hwT_hi_done = sem("hwT_hi_done")
        hwT_lo_done = sem("hwT_lo_done")
        out_mm = sem("out_mm")
        out_done = sem("out_done")
        OUT_CREDIT = 2
        ROUTE_STEPS = 8
        MIX_STEPS = 3

        arT_cols = arT.rearrange("(c p) n -> p c n", p=P)
        weights = [(wT_chunks[c], w_hi[:, c, :], w_lo[:, c, :]) for c in range(DC)]
        weights += [(arT_cols, ar_hi[:].rearrange("p c n -> p (c n)"), ar_lo[:].rearrange("p c n -> p (c n)")),
                    (bT, b_hi[:], b_lo[:])]

        def staged(n):
            return w_stage[:, n % STAGE, 0:DC * AR if n == DC else D]

        def over_tiles(eng, tile):
            with eng.Fori(0, TILES // SLOTS - 1) as turn:
                for s in range(SLOTS):
                    tile(turn * SLOTS + s, s, SLOTS, turn)
            for s in range(SLOTS):
                tile(TILES - SLOTS + s, s, SLOTS - 1 - s, TILES // SLOTS - 1)

        def moved(turn):
            return turn * 16 + 16

        block = ctx.enter_context(nc.Block())

        @block.sync
        def _(sp):
            for s in range(2):
                sp.dma_start(x_sb[:, s, :], x_tiles[s]).then_inc(x_in[s], 16)
            for n, (src, _, _) in enumerate(weights):
                if n == STAGE:
                    for s in range(2, SLOTS):
                        sp.dma_start(x_sb[:, s, :], x_tiles[s]).then_inc(x_in[s], 16)
                if n >= STAGE:
                    sp.wait_ge(w_lo_done, n - STAGE + 1)
                dst = staged(n)
                if n == DC:
                    dst = dst.rearrange("p (c n) -> p c n", c=DC)
                sp.dma_start(dst, src).then_inc(w_in[n % STAGE], 16)

            def tile(t, s, ahead, turn):
                sp.wait_ge(out_done, t + 1 + OUT_CREDIT)
                sp.dma_start(out_tiles[t], x_sb[:, s, :]).then_inc(stored[s], 16)
                if ahead >= SLOTS:
                    sp.wait_ge(stored[s], moved(turn))
                    sp.dma_start(x_sb[:, s, :], x_tiles[t + SLOTS]).then_inc(x_in[s], 16)

            over_tiles(sp, tile)
            for s in range(SLOTS):
                sp.wait_ge(stored[s], 16 * (TILES // SLOTS))

        @block.tensor
        def _(pe):
            def split_products(dst, terms, first, last):
                for n, (stat, mov) in enumerate(terms):
                    mm = nc.tensor.matmul(dst, stat, mov, start=first and n == 0,
                                          stop=last and n == len(terms) - 1)
                return mm

            def y_products():
                for c in range(DC):
                    cols = slice(c * P, (c + 1) * P)
                    mm = split_products(ps_y[:, cols], [
                        (x_hi[:, cols], mix_hi[:]), (x_hi[:, cols], mix_lo[:]),
                        (x_lo[:, cols], mix_hi[:])], True, True)
                mm.then_inc(y_mm, 1)

            pe.wait_ge(cond_in, 16 * 7)
            nc.tensor.matmul(ps_ar[:, 0:BATCH], w0_sb[:], condT_sb[:], start=True, stop=True).then_inc(cond_mm, 1)
            pe.wait_ge(gelu_done, 1)
            nc.tensor.matmul(ps_hwT[:, 0:BATCH], w1_sb[:], h1T[:], start=True, stop=True).then_inc(cond_mm, 1)
            pe.wait_ge(gelu_done, 2)
            nc.tensor.matmul(ps_ar[:, 0:KERNELS], h2T[:], w2_sb[:], start=True, stop=True).then_inc(cond_mm, 1)
            pe.wait_ge(consts_in, 32)
            pe.wait_ge(att_step, 5)
            nc.tensor.matmul(ps_hwT[0:PAIR * KERNELS, 0:TILES], att_par[:], pair_sel, start=True, stop=True).then_inc(cond_mm, 1)
            nc.tensor.matmul(ps_ar[0:KERNELS, 0:BATCH], att[:], ident, start=True, stop=True).then_inc(cond_mm, 1)
            pe.wait_ge(att_step, 6)
            pe.wait_ge(mixw_in, 16)
            for g in range(CH // O_BANK):
                if g >= 4:
                    pe.wait_ge(agg_done, g - 3)
                for j in range(O_BANK):
                    mm = nc.tensor.matmul(ps_agg[g % 4][:, j * TILES:(j + 1) * TILES],
                                          mixw[:, g * O_BANK + j, :], attT_par[:], start=True, stop=True)
                mm.then_inc(agg_mm, 1)
                if g == 0:
                    pe.wait_ge(att_step, 7)
                    nc.tensor.matmul(ps_hwT[:, P:P + CH], attT[:], mix_b_sb[:], start=True, stop=True).then_inc(cond_mm, 1)

            pe.wait_ge(x_hi_done, 1)
            pe.wait_ge(x_lo_done, 1)
            pe.wait_ge(mix_done, 1)
            y_products()
            pe.wait_ge(w_hi_done, len(weights))
            pe.wait_ge(w_lo_done, len(weights))

            def tile(t, s, ahead, turn):
                u = s % 2
                if ahead >= 1:
                    pe.wait_ge(x_hi_done, t + 2)
                    pe.wait_ge(x_lo_done, t + 2)
                    pe.wait_ge(mix_done, t + 2)
                    pe.wait_ge(y_summed, t + 1)
                    y_products()
                pe.wait_ge(y_hi_done, t + 1)
                pe.wait_ge(y_lo_done, t + 1)
                pe.wait_ge(out_done, t + 1)
                for c in range(DC):
                    cols = slice(c * P, (c + 1) * P)
                    hi, lo = y_hi[:, u, cols], y_lo[:, u, cols]
                    split_products(ps_out[:, u, 0:HALF], [
                        (hi, w_hi[:, c, 0:HALF]), (hi, w_lo[:, c, 0:HALF])], c == 0, False)
                    split_products(ps_ar[:, 0:AR], [
                        (hi, ar_hi[:, c, :]), (hi, ar_lo[:, c, :])], c == 0, False)
                    split_products(ps_out[:, u, 0:HALF], [(lo, w_hi[:, c, 0:HALF])], False, False)
                    mm = split_products(ps_ar[:, 0:AR], [(lo, ar_hi[:, c, :])], False, c == DC - 1)
                mm.then_inc(ar_mm, 1)
                for c in range(DC):
                    cols = slice(c * P, (c + 1) * P)
                    hi, lo = y_hi[:, u, cols], y_lo[:, u, cols]
                    if c == DC - 2:
                        pe.wait_ge(hw_done, t + 1)
                        nc.tensor.transpose(ps_hwT[:, 0:P], hw[:], ident).then_inc(hwT_mm, 1)
                    split_products(ps_out[:, u, HALF:D], [
                        (hi, w_hi[:, c, HALF:D]), (hi, w_lo[:, c, HALF:D]),
                        (lo, w_hi[:, c, HALF:D])], c == 0, False)
                pe.wait_ge(hwT_hi_done, t + 1)
                for n in range(2):
                    half = slice(n * HALF, (n + 1) * HALF)
                    split_products(ps_out[:, u, half], [(hwT_hi[:], b_hi[:, half]), (hwT_hi[:], b_lo[:, half])],
                                   False, False)
                pe.wait_ge(hwT_lo_done, t + 1)
                for n in range(2):
                    half = slice(n * HALF, (n + 1) * HALF)
                    mm = split_products(ps_out[:, u, half], [(hwT_lo[:], b_hi[:, half])], False, True)
                mm.then_inc(out_mm, 1)

            over_tiles(pe, tile)

        @block.scalar
        def _(act):
            act.dma_start(condT_sb[:], condT).then_inc(cond_in, 16)
            act.dma_start(w0_sb[:], w0).then_inc(cond_in, 16)
            act.dma_start(b0_sb[:], b0).then_inc(cond_in, 16)
            act.dma_start(w1_sb[:], w1).then_inc(cond_in, 16)
            act.dma_start(b1_sb[:], b1).then_inc(cond_in, 16)
            act.dma_start(w2_sb[:], w2).then_inc(cond_in, 16)
            act.dma_start(mix_b_sb[:], mix_b).then_inc(cond_in, 16)
            act.dma_start(b2_sb[:], b2.partition_broadcast(P)).then_inc(consts_in, 16)
            act.dma_start(consts_sb[:], consts).then_inc(consts_in, 16)
            act.dma_start(mixw, mix_w).then_inc(mixw_in, 16)
            act.dma_start(bias_out[:], b_base.partition_broadcast(P)).then_inc(bias_out_in, 16)

            act.wait_ge(cond_mm, 1)
            nc.scalar.activation(h1T[:], ps_ar[:, 0:BATCH], ACT.Gelu, bias=b0_sb[:, 0:1]).then_inc(gelu_done, 1)
            act.wait_ge(cond_mm, 2)
            nc.scalar.activation(h2T[:], ps_hwT[:, 0:BATCH], ACT.Gelu, bias=b1_sb[:, 0:1]).then_inc(gelu_done, 1)
            act.wait_ge(att_step, 2)
            nc.scalar.activation(score_exp[:], score[:], ACT.Exp, bias=neg_max[:, 0:1],
                                 accum_out=exp_sum[:, 0:1]).then_inc(score_exped, 1)
            def split_weight(n):
                act.wait_ge(w_in[n % STAGE], 16 * (n // STAGE + 1))
                nc.scalar.copy(weights[n][1], staged(n)).then_inc(w_hi_done, 1)

            act.wait_ge(att_step, 8)
            act.dma_start(agg_b_dram, agg_b_rows[:]).then_inc(agg_b_out, 16)
            act.wait_ge(x_in[0], 16)
            nc.scalar.copy(x_hi[:], x_sb[:, 0, :]).then_inc(x_hi_done, 1)
            for n in range(2):
                split_weight(n)
            act.wait_ge(agg_b_out, 16)
            act.wait_ge(agg_mm, CH // O_BANK)
            agg_b_flat = agg_b_dram.rearrange("b c -> (b c)")
            first = SLOTS * P
            act.dma_start(agg_b[:, 0:first], agg_b_flat[0:first].partition_broadcast(P)).then_inc(agg_b_in[0], 16)
            act.dma_start(agg_b[:, first:], agg_b_flat[first:].partition_broadcast(P)).then_inc(agg_b_in[1], 16)
            for n in range(2, 6):
                split_weight(n)

            act.wait_ge(y_summed, 1)
            nc.scalar.copy(y_hi[:, 0, :], y_sb[:]).then_inc(y_hi_done, 1)
            act.wait_ge(x_in[1], 16)
            act.wait_ge(y_mm, 1)
            nc.scalar.copy(x_hi[:], x_sb[:, 1, :]).then_inc(x_hi_done, 1)
            for n in range(6, len(weights)):
                split_weight(n)

            def tile(t, s, ahead, turn):
                if ahead >= 1:
                    act.wait_ge(y_summed, t + 2)
                    nc.scalar.copy(y_hi[:, (s + 1) % 2, :], y_sb[:]).then_inc(y_hi_done, 1)
                if ahead >= 2:
                    n = (s + 2) % SLOTS
                    act.wait_ge(x_in[n], moved(turn + (s + 2) // SLOTS))
                    act.wait_ge(y_mm, t + 2)
                    nc.scalar.copy(x_hi[:], x_sb[:, n, :]).then_inc(x_hi_done, 1)
                act.wait_ge(routed, ROUTE_STEPS * t + 3)
                nc.scalar.activation(ratio[:], top_gap[:], ACT.Exp).then_inc(ratio_done, 1)
                act.wait_ge(hwT_mm, t + 1)
                nc.scalar.copy(hwT_hi[:], ps_hwT[:, 0:P]).then_inc(hwT_hi_done, 1)

            over_tiles(act, tile)

        @block.gpsimd
        def _(pool):
            def split_weight(n):
                pool.wait_ge(w_hi_done, n + 1)
                nc.gpsimd.tensor_tensor(weights[n][2], staged(n), weights[n][1].bitcast(F32),
                                        ALU.subtract).then_inc(w_lo_done, 1)

            def mix_parts(t):
                nc.gpsimd.tensor_copy(mix_pair[:], agg_w[:, t, :]).then_inc(mix_step, 1)
                blocks = mix_pair[:].unsqueeze(1).to_broadcast([P, PAIR, CH])
                pool.wait_ge(mix_step, MIX_STEPS * t + 1)
                for part in (mix_f32, mix_hi):
                    nc.gpsimd.tensor_tensor(part[:].rearrange("p (s o) -> p s o", s=PAIR), blocks, diagonal,
                                            ALU.mult).then_inc(mix_step, 1)
                pool.wait_ge(mix_step, MIX_STEPS * t + 3)
                nc.gpsimd.tensor_tensor(mix_lo[:], mix_f32[:], mix_hi[:].bitcast(F32),
                                        ALU.subtract).then_inc(mix_done, 1)

            for n in range(2):
                split_weight(n)
            pool.wait_ge(consts_in, 32)
            pool.wait_ge(agg_done, CH // O_BANK)
            mix_parts(0)
            for n in range(2, 6):
                split_weight(n)
            pool.wait_ge(y_mm, 1)
            mix_parts(1)
            for n in range(6, len(weights)):
                split_weight(n)
            pool.wait_ge(bias_out_in, 16)
            pool.wait_ge(x_hi_done, 1)
            pool.wait_ge(x_lo_done, 1)
            nc.gpsimd.tensor_tensor(x_sb[:, 0, :], x_sb[:, 0, :], bias_out[:], ALU.add).then_inc(x_biased, 1)

            def tile(t, s, ahead, turn):
                if ahead >= 2:
                    pool.wait_ge(y_mm, t + 2)
                    mix_parts(t + 2)
                if ahead >= 1:
                    n = (s + 1) % SLOTS
                    pool.wait_ge(x_hi_done, t + 2)
                    pool.wait_ge(x_lo_done, t + 2)
                    nc.gpsimd.tensor_tensor(x_sb[:, n, :], x_sb[:, n, :], bias_out[:],
                                            ALU.add).then_inc(x_biased, 1)

            over_tiles(pool, tile)

        @block.vector
        def _(dve):
            dve.wait_ge(cond_mm, 3)
            dve.wait_ge(consts_in, 32)
            nc.vector.tensor_tensor(score[:], ps_ar[:, 0:KERNELS], b2_sb[:], ALU.add).then_inc(att_step, 1)
            dve.wait_ge(att_step, 1)
            nc.vector.tensor_reduce(neg_max[:], score[:], AX_X, ALU.max, negate=True).then_inc(att_step, 1)
            dve.wait_ge(score_exped, 1)
            nc.vector.reciprocal(exp_inv[:], exp_sum[:]).then_inc(att_step, 1)
            dve.wait_ge(att_step, 3)
            nc.vector.tensor_scalar(att[:], score_exp[:], exp_inv[:, 0:1], None, ALU.mult).then_inc(att_step, 1)
            dve.wait_ge(att_step, 4)
            nc.vector.tensor_tensor(att_par[:].rearrange("p (s k) -> p s k", s=PAIR),
                                    att[:].unsqueeze(1).to_broadcast([P, PAIR, KERNELS]),
                                    parity.rearrange("p (s k) -> p s k", s=PAIR), ALU.mult).then_inc(att_step, 1)
            dve.wait_ge(cond_mm, 4)
            nc.vector.tensor_copy(attT_par[:], ps_hwT[0:PAIR * KERNELS, 0:TILES]).then_inc(att_step, 1)
            dve.wait_ge(cond_mm, 5)
            nc.vector.tensor_copy(attT[:], ps_ar[0:KERNELS, 0:BATCH]).then_inc(att_step, 1)
            dve.wait_ge(cond_mm, 6)
            nc.vector.tensor_copy(agg_b_rows[:], ps_hwT[:, P:P + CH]).then_inc(att_step, 1)

            def x_low(slot):
                nc.vector.tensor_tensor(x_lo[:], x_sb[:, slot, :], x_hi[:].bitcast(F32),
                                        ALU.subtract).then_inc(x_lo_done, 1)

            def y_sum(t):
                nc.vector.tensor_tensor(
                    y_sb[:].rearrange("p (c n) -> p c n", c=DC), ps_y[:].rearrange("p (c n) -> p c n", c=DC),
                    agg_b[:, bass.ts(t, P)].unsqueeze(1).to_broadcast([P, DC, P]), ALU.add).then_inc(y_summed, 1)

            def y_low(u):
                nc.vector.tensor_tensor(y_lo[:, u, :], y_sb[:], y_hi[:, u, :].bitcast(F32),
                                        ALU.subtract).then_inc(y_lo_done, 1)

            for g in range(CH // O_BANK):
                if g == 1:
                    dve.wait_ge(x_hi_done, 1)
                    x_low(0)
                dve.wait_ge(agg_mm, g + 1)
                nc.vector.tensor_copy(agg_w[:, :, g * O_BANK:(g + 1) * O_BANK].rearrange("p t o -> p o t"),
                                      ps_agg[g % 4].rearrange("p (o t) -> p o t", o=O_BANK)).then_inc(agg_done, 1)
            dve.wait_ge(y_mm, 1)
            dve.wait_ge(agg_b_in[0], 16)
            y_sum(0)
            dve.wait_ge(y_hi_done, 1)
            y_low(0)
            dve.wait_ge(x_hi_done, 2)
            x_low(1)
            dve.wait_ge(agg_b_in[1], 16)
            nc.vector.memset(half_sum[:], 0.0).then_inc(out_done, OUT_CREDIT)

            def tile(t, s, ahead, turn):
                u = s % 2
                if ahead >= 1:
                    dve.wait_ge(y_mm, t + 2)
                    dve.wait_ge(y_lo_done, t + 1)
                    y_sum(t + 1)
                    dve.wait_ge(y_hi_done, t + 2)
                    y_low(1 - u)
                if ahead >= 2:
                    dve.wait_ge(x_hi_done, t + 3)
                    x_low((s + 2) % SLOTS)
                step = ROUTE_STEPS * t
                logits = ps_ar[:, ER:AR]
                dve.wait_ge(ar_mm, t + 1)
                nc.vector.tensor_copy(logits_sb[:], logits).then_inc(routed, 1)
                nc.vector.max(top_val[:], logits).then_inc(routed, 1)
                dve.wait_ge(routed, step + 2)
                nc.vector.tensor_tensor(top_gap[:], top_val[:, 1:2], top_val[:, 0:1],
                                        ALU.subtract).then_inc(routed, 1)
                nc.vector.max_index(top_idx[:], top_val[:], logits_sb[:]).then_inc(routed, 1)
                dve.wait_ge(routed, step + 4)
                nc.vector.tensor_tensor(picked[:], expert_no,
                                        top_idx[:, 0:2].unsqueeze(2).to_broadcast([P, 2, EXPERTS]),
                                        ALU.is_equal).then_inc(routed, 1)
                dve.wait_ge(ratio_done, t + 1)
                nc.vector.tensor_scalar(half_sum[:], ratio[:], 1.0 / LORA_SCALE, 1.0 / LORA_SCALE,
                                        ALU.mult, ALU.add).then_inc(routed, 1)
                dve.wait_ge(routed, step + 5)
                nc.vector.scalar_tensor_tensor(expert_w[:], picked[:, 1, :], ratio[:, 0:1], picked[:, 0, :],
                                               ALU.mult, ALU.add).then_inc(routed, 1)
                dve.wait_ge(routed, step + 6)
                nc.vector.reciprocal(first_w[:], half_sum[:]).then_inc(routed, 1)
                dve.wait_ge(routed, step + 8)
                nc.vector.scalar_tensor_tensor(
                    hw[:].rearrange("p (e r) -> p e r", e=EXPERTS),
                    ps_ar[:, 0:ER].rearrange("p (e r) -> p e r", e=EXPERTS), first_w[:, 0:1],
                    expert_w[:].unsqueeze(2).to_broadcast([P, EXPERTS, RANK]), ALU.mult, ALU.mult).then_inc(hw_done, 1)
                dve.wait_ge(hwT_hi_done, t + 1)
                nc.vector.tensor_tensor(hwT_lo[:], ps_hwT[:, 0:P], hwT_hi[:].bitcast(F32),
                                        ALU.subtract).then_inc(hwT_lo_done, 1)
                dve.wait_ge(out_mm, t + 1)
                dve.wait_ge(x_biased, t + 1)
                nc.vector.tensor_tensor(x_sb[:, s, :], ps_out[:, u, :], x_sb[:, s, :], ALU.add).then_inc(out_done, 1)

            over_tiles(dve, tile)


def kernel(x, cond_128, L0_cond_W0, L0_cond_b0, L0_cond_W1, L0_cond_b1, L0_cond_W2, L0_cond_b2,
           L0_cond_weight, L0_cond_bias_k, L0_ffn_W_base, L0_ffn_b_base, L0_ffn_W_router, L0_ffn_A, L0_ffn_B):
    import concourse.bacc as bacc
    from concourse.bass_utils import run_bass_kernel_spmd

    def lay(a):
        return np.ascontiguousarray(a)

    x = np.asarray(x)
    mix = np.asarray(L0_cond_weight)[..., 0]
    mix_w = np.zeros((PAIR, KERNELS, CH, PAIR, CH), mix.dtype)
    for par in range(PAIR):
        mix_w[par, :, :, par, :] = mix
    ar = np.concatenate([np.asarray(L0_ffn_A).reshape(ER, D), np.asarray(L0_ffn_W_router)], axis=0)
    arrays = {
        "x": lay(x.reshape(BATCH * CH, D)),
        "condT": lay(np.asarray(cond_128).T),
        "w0": lay(L0_cond_W0), "b0": lay(np.asarray(L0_cond_b0).reshape(HID, 1)),
        "w1": lay(L0_cond_W1), "b1": lay(np.asarray(L0_cond_b1).reshape(HID, 1)),
        "w2": lay(L0_cond_W2), "b2": lay(L0_cond_b2),
        "mix_w": lay(mix_w.reshape(PAIR * KERNELS, CH, P)), "mix_b": lay(L0_cond_bias_k),
        "wT": lay(np.asarray(L0_ffn_W_base).T), "b_base": lay(L0_ffn_b_base),
        "arT": lay(ar.T),
        "bT": lay(np.asarray(L0_ffn_B).transpose(0, 2, 1).reshape(ER, D)),
        "consts": shape_constants(),
    }
    nc = bacc.Bacc("TRN2", target_bir_lowering=False, num_devices=1)
    ins = [nc.dram_tensor("in_" + name, a.shape, mybir.dt.from_np(a.dtype), kind="ExternalInput").ap()
           for name, a in arrays.items()]
    out = nc.dram_tensor("result", (BATCH * CH, D), F32, kind="ExternalOutput").ap()
    build(nc, *ins, out)
    run = run_bass_kernel_spmd(nc, [{"in_" + name: a for name, a in arrays.items()}], core_ids=[0])
    return run.results[0]["result"].reshape(x.shape)
```

```python
from contextlib import ExitStack

import numpy as np

import concourse.bass as bass
from concourse import mybir

ALU = mybir.AluOpType
ACT = mybir.ActivationFunctionType
F32 = mybir.dt.float32
F32R = mybir.dt.float32r
U32 = mybir.dt.uint32
AX_X = mybir.AxisListType.X

P = 128
BATCH, CH, D = 128, 64, 1024
HID = 128
KERNELS = 8
EXPERTS, RANK = 8, 16
ER = EXPERTS * RANK
PAIR = P // CH
TILES = BATCH // PAIR
DC = D // P
BANK = 512
AR = ER + EXPERTS
WIDE = AR + D
CUTS = (0, 384, 772, WIDE)
SLOTS = 4
STAGE = 4
LORA_SCALE = 2.0
HALVES = 2
HC = DC // HALVES
HD = D // HALVES

SMALL = {}
_at = 0
for _name, _width in (("condT", BATCH), ("w0", HID), ("b0", 1), ("w1", HID), ("b1", 1), ("w2", KERNELS),
                      ("b2", KERNELS), ("mix_b", CH), ("ident", P), ("expert_no", 2 * EXPERTS)):
    SMALL[_name] = slice(_at, _at + _width)
    _at += _width
SMALL_COLS = _at


def out_columns(piece):
    first = max(CUTS[piece], AR)
    return slice(first - AR, CUTS[piece + 1] - AR), slice(first - CUTS[piece], CUTS[piece + 1] - CUTS[piece])


def build(nc, x, small, mix_w, wide, b_base, bT, out):
    x_tiles = x.rearrange("(t p) h -> t p h", p=P)
    out_tiles = out.rearrange("(t p) h -> t p h", p=P)
    agg_w_dram = nc.dram_tensor("agg_w_rows", (BATCH * CH, CH), F32, kind="Internal").ap()
    agg_b_dram = nc.dram_tensor("agg_b_rows", (BATCH * CH,), F32, kind="Internal").ap()
    agg_w_pairs = agg_w_dram.rearrange("(t p) o -> t p o", p=P)
    agg_b_pairs = agg_b_dram.rearrange("(t n) -> t n", n=P)

    with ExitStack() as ctx:
        def sb(name, shape, dt=F32):
            return ctx.enter_context(nc.sbuf_tensor(name, shape, dt))

        def sem(name):
            return ctx.enter_context(nc.semaphore(name))

        w_hi = sb("w_hi", [P, DC, WIDE], F32R)
        w_lo = sb("w_lo", [P, DC, WIDE], F32R)
        b_hi = sb("b_hi", [P, D], F32R)
        b_lo = sb("b_lo", [P, D], F32R)
        bias_out = sb("bias_out", [P, D])
        x_sb = sb("x_sb", [P, SLOTS, D])
        x_hi = sb("x_hi", [P, D], F32R)
        x_lo = sb("x_lo", [P, D], F32R)
        mix = sb("mix", [P, SLOTS, P])
        mix_parts = sb("mix_parts", [P, 2 * P], F32R)
        bias_y = sb("bias_y", [P, SLOTS, P])
        y_sb = sb("y_sb", [P, D])
        y_hi = sb("y_hi", [P, 2, D], F32R)
        y_lo = sb("y_lo", [P, 2, D], F32R)
        logits_sb = sb("logits_sb", [P, EXPERTS])
        top_val = sb("top_val", [P, 8])
        top_gap = sb("top_gap", [P, 1])
        top_idx = sb("top_idx", [P, 8], U32)
        picked = sb("picked", [P, 2, EXPERTS])
        ratio = sb("ratio", [P, 1])
        scaled_sum = sb("scaled_sum", [P, 1])
        first_w = sb("first_w", [P, 1])
        expert_w = sb("expert_w", [P, EXPERTS])
        hw = sb("hw", [P, ER])
        hwT_hi = sb("hwT_hi", [P, P], F32R)
        hwT_lo = sb("hwT_lo", [P, P], F32R)
        small_sb = sb("small_sb", [P, SMALL_COLS])
        mix_w_sb = sb("mix_w_sb", [KERNELS, CH * CH])
        w_stage = sb("w_stage", [P, STAGE, WIDE])
        h1T = sb("h1T", [P, BATCH])
        h2T = sb("h2T", [P, BATCH])
        score = sb("score", [P, KERNELS])
        neg_max = sb("neg_max", [P, 1])
        score_exp = sb("score_exp", [P, KERNELS])
        exp_sum = sb("exp_sum", [P, 1])
        exp_inv = sb("exp_inv", [P, 1])
        att = sb("att", [P, KERNELS])
        attT = sb("attT", [KERNELS, BATCH])
        agg_w = sb("agg_w", [BATCH, CH * CH])
        agg_b = sb("agg_b", [BATCH, CH])

        ident = small_sb[:, SMALL["ident"]]
        expert_no = small_sb[:, SMALL["expert_no"]].rearrange("p (s e) -> p s e", s=2)

        ps_main = ctx.enter_context(nc.psum_tensor("ps_main", [P, 2, 3, BANK], F32))
        ps_y = ctx.enter_context(nc.psum_tensor("ps_y", [P, HC, 2, P], F32))
        ps_y_flat = ps_y[:].rearrange("p c k n -> p (c k n)")

        small_in = sem("small_in")
        mix_w_in = sem("mix_w_in")
        w_in = [sem(f"w_in{s}") for s in range(STAGE)]
        bias_out_in = sem("bias_out_in")
        cond_mm = sem("cond_mm")
        gelu_done = sem("gelu_done")
        att_step = sem("att_step")
        score_exped = sem("score_exped")
        agg_b_mm = sem("agg_b_mm")
        agg_b_done = sem("agg_b_done")
        agg_mm = sem("agg_mm")
        agg_done = sem("agg_done")
        agg_b_out = sem("agg_b_out")
        agg_w_out = sem("agg_w_out")
        mix_zeroed = sem("mix_zeroed")
        w_hi_done = sem("w_hi_done")
        w_lo_done = [sem("w_lo_done_dve"), sem("w_lo_done_pool")]
        x_in = [sem(f"x_in{s}") for s in range(SLOTS)]
        mix_in = [sem(f"mix_in{s}") for s in range(SLOTS)]
        bias_y_in = [sem(f"bias_y_in{s}") for s in range(SLOTS)]
        stored = [sem(f"stored{s}") for s in range(SLOTS)]
        x_hi_done = sem("x_hi_done")
        x_lo_done = sem("x_lo_done")
        x_biased = sem("x_biased")
        mix_hi_done = sem("mix_hi_done")
        mix_lo_done = sem("mix_lo_done")
        y_mm = sem("y_mm")
        y_part = sem("y_part")
        y_summed = sem("y_summed")
        y_hi_done = sem("y_hi_done")
        y_lo_done = sem("y_lo_done")
        ar_mm = sem("ar_mm")
        routed = sem("routed")
        ratio_done = sem("ratio_done")
        hw_done = sem("hw_done")
        hwT_mm = sem("hwT_mm")
        hwT_hi_done = sem("hwT_hi_done")
        hwT_lo_done = sem("hwT_lo_done")
        out_mm = sem("out_mm")
        out_done = sem("out_done")
        ROUTE_STEPS = 8

        wide_chunks = wide.rearrange("(c p) n -> c p n", p=P)
        weights = [(wide_chunks[c], w_hi[:, c, :], w_lo[:, c, :]) for c in range(DC)]
        weights += [(bT, b_hi[:], b_lo[:])]

        def staged(n):
            return w_stage[:, n % STAGE, 0:WIDE if n < DC else D]

        def over_tiles(eng, tile):
            with eng.Fori(0, TILES // SLOTS - 1) as turn:
                for s in range(SLOTS):
                    tile(turn * SLOTS + s, s, SLOTS, turn)
            for s in range(SLOTS):
                tile(TILES - SLOTS + s, s, SLOTS - 1 - s, TILES // SLOTS - 1)

        def moved(turn, dmas=1):
            return turn * (16 * dmas) + 16 * dmas

        def halves(t, g):
            return t * HALVES + g + 1

        block = ctx.enter_context(nc.Block())

        @block.sync
        def _(sp):
            def load_mix(s, rows):
                for par in range(PAIR):
                    blk = slice(par * CH, (par + 1) * CH)
                    sp.dma_start(mix[blk, s, blk], rows[blk, :]).then_inc(mix_in[s], 16)

            def load_bias_y(s, t):
                sp.dma_start(bias_y[:, s, :], agg_b_pairs[t].partition_broadcast(P)).then_inc(bias_y_in[s], 16)

            sp.dma_start(small_sb[:], small).then_inc(small_in, 16)
            sp.dma_start(mix_w_sb[:], mix_w).then_inc(mix_w_in, 16)
            for n, (src, _, _) in enumerate(weights):
                if n in (2, 3):
                    sp.dma_start(x_sb[:, n - 2, :], x_tiles[n - 2]).then_inc(x_in[n - 2], 16)
                if n >= STAGE:
                    before = n - STAGE
                    sp.wait_ge(w_lo_done[before % 2], before // 2 + 1)
                sp.dma_start(staged(n), src).then_inc(w_in[n % STAGE], 16)
            sp.dma_start(bias_out[:], b_base.partition_broadcast(P)).then_inc(bias_out_in, 16)
            sp.wait_ge(agg_b_done, 1)
            sp.dma_start(agg_b_dram.rearrange("(b o) -> b o", b=BATCH), agg_b[:]).then_inc(agg_b_out, 16)
            sp.wait_ge(mix_zeroed, 1)
            sp.wait_ge(agg_done, CH * CH // BANK)
            for t in range(2):
                for par in range(PAIR):
                    b, blk = t * PAIR + par, slice(par * CH, (par + 1) * CH)
                    sp.dma_start(mix[blk, t, blk], agg_w[b:b + 1, :].rearrange("b (i o) -> b i o", i=CH)
                                 ).then_inc(mix_in[t], 16)
            sp.wait_ge(agg_b_out, 16)
            for t in range(SLOTS):
                load_bias_y(t, t)
            sp.dma_start(agg_w_dram.rearrange("(b i) o -> b (i o)", b=BATCH), agg_w[:]).then_inc(agg_w_out, 16)
            for s in range(2, SLOTS):
                sp.dma_start(x_sb[:, s, :], x_tiles[s]).then_inc(x_in[s], 16)
            sp.wait_ge(agg_w_out, 16)
            for t in range(2, SLOTS):
                load_mix(t, agg_w_pairs[t])

            def tile(t, s, ahead, turn):
                sp.wait_ge(out_done, t + 1)
                sp.dma_start(out_tiles[t], x_sb[:, s, :]).then_inc(stored[s], 16)
                if ahead >= SLOTS:
                    load_mix(s, agg_w_pairs[t + SLOTS])
                    load_bias_y(s, t + SLOTS)
                    sp.wait_ge(stored[s], moved(turn))
                    sp.dma_start(x_sb[:, s, :], x_tiles[t + SLOTS]).then_inc(x_in[s], 16)

            over_tiles(sp, tile)
            for s in range(SLOTS):
                sp.wait_ge(stored[s], 16 * (TILES // SLOTS))

        @block.tensor
        def _(pe):
            def y_products(g):
                for j in range(HC):
                    cols = slice((g * HC + j) * P, (g * HC + j + 1) * P)
                    nc.tensor.matmul(ps_y[:, j, :, :].rearrange("p k n -> p (k n)"), x_hi[:, cols], mix_parts[:],
                                     start=True, stop=False)
                    mm = nc.tensor.matmul(ps_y[:, j, 0, :], x_lo[:, cols], mix_parts[:, 0:P],
                                          start=False, stop=True)
                mm.then_inc(y_mm, 1)

            def piece_products(u, k, c):
                cols, piece = slice(c * P, (c + 1) * P), slice(CUTS[k], CUTS[k + 1])
                dst = ps_main[:, u, k, 0:CUTS[k + 1] - CUTS[k]]
                nc.tensor.matmul(dst, y_hi[:, u, cols], w_hi[:, c, piece], start=c == 0, stop=False)
                nc.tensor.matmul(dst, y_hi[:, u, cols], w_lo[:, c, piece], start=False, stop=False)
                return nc.tensor.matmul(dst, y_lo[:, u, cols], w_hi[:, c, piece], start=False, stop=c == DC - 1)

            def expert_products(u, stat, mov):
                for k in range(3):
                    res, at = out_columns(k)
                    mm = nc.tensor.matmul(ps_main[:, u, k, at], stat[:], mov[:, res], start=False, stop=True,
                                          skip_group_check=True)
                return mm

            def chain(dst, stat, mov, done):
                nc.tensor.matmul(dst, stat, mov, start=True, stop=True).then_inc(done, 1)

            pe.wait_ge(small_in, 16)
            chain(ps_y_flat[:, 0:BATCH], small_sb[:, SMALL["w0"]], small_sb[:, SMALL["condT"]], cond_mm)
            pe.wait_ge(gelu_done, 1)
            chain(ps_y_flat[:, BANK:BANK + BATCH], small_sb[:, SMALL["w1"]], h1T[:], cond_mm)
            pe.wait_ge(gelu_done, 2)
            chain(ps_y_flat[:, 0:KERNELS], h2T[:], small_sb[:, SMALL["w2"]], cond_mm)
            pe.wait_ge(att_step, 4)
            chain(ps_y_flat[0:KERNELS, BANK:BANK + BATCH], att[:], ident, cond_mm)
            pe.wait_ge(att_step, 5)
            chain(ps_y_flat[:, 0:CH], attT[:], small_sb[0:KERNELS, SMALL["mix_b"]], agg_b_mm)
            pe.wait_ge(mix_w_in, 16)
            for g in range(CH * CH // BANK):
                if g >= 6:
                    pe.wait_ge(agg_done, g - 5)
                chain(ps_main[:, g // 3 % 2, g % 3, :], attT[:], mix_w_sb[:, g * BANK:(g + 1) * BANK], agg_mm)

            pe.wait_ge(agg_b_done, 1)
            pe.wait_ge(x_hi_done, 1)
            pe.wait_ge(x_lo_done, 1)
            pe.wait_ge(mix_hi_done, 1)
            pe.wait_ge(mix_lo_done, 1)
            y_products(0)
            pe.wait_ge(y_summed, 1)
            y_products(1)
            pe.wait_ge(agg_done, CH * CH // BANK)
            for n in range(2):
                pe.wait_ge(w_lo_done[n], (len(weights) + 1 - n) // 2)

            def tile(t, s, ahead, turn):
                u = s % 2
                if ahead >= 1:
                    pe.wait_ge(x_hi_done, t + 2)
                    pe.wait_ge(x_lo_done, t + 2)
                    pe.wait_ge(mix_hi_done, t + 2)
                    pe.wait_ge(mix_lo_done, t + 2)
                    pe.wait_ge(y_summed, halves(t, 1))
                    y_products(0)
                pe.wait_ge(y_hi_done, halves(t, 1))
                pe.wait_ge(y_lo_done, halves(t, 1))
                for c in range(DC):
                    mm = piece_products(u, 0, c)
                mm.then_inc(ar_mm, 1)
                if ahead >= 1:
                    pe.wait_ge(y_summed, halves(t + 1, 0))
                    y_products(1)
                for c in range(DC):
                    piece_products(u, 1, c)
                for c in range(DC):
                    if c == DC - 2:
                        pe.wait_ge(hw_done, t + 1)
                        nc.tensor.transpose(ps_main[:, 1 - u, 0, 0:P], hw[:], ident).then_inc(hwT_mm, 1)
                    piece_products(u, 2, c)
                pe.wait_ge(hwT_hi_done, t + 1)
                expert_products(u, hwT_hi, b_hi)
                expert_products(u, hwT_hi, b_lo)
                pe.wait_ge(hwT_lo_done, t + 1)
                expert_products(u, hwT_lo, b_hi).then_inc(out_mm, 1)

            over_tiles(pe, tile)

        @block.scalar
        def _(act):
            def split_weight(n):
                act.wait_ge(w_in[n % STAGE], 16 * (n // STAGE + 1))
                nc.scalar.copy(weights[n][1], staged(n)).then_inc(w_hi_done, 1)

            def x_high(s):
                nc.scalar.copy(x_hi[:], x_sb[:, s, :]).then_inc(x_hi_done, 1)

            def mix_high(s):
                nc.scalar.copy(mix_parts[:, 0:P], mix[:, s, :]).then_inc(mix_hi_done, 1)

            def y_high(u, g):
                half = slice(g * HD, (g + 1) * HD)
                nc.scalar.copy(y_hi[:, u, half], y_sb[:, half]).then_inc(y_hi_done, 1)

            act.wait_ge(cond_mm, 1)
            nc.scalar.activation(h1T[:], ps_y_flat[:, 0:BATCH], ACT.Gelu,
                                 bias=small_sb[:, SMALL["b0"]]).then_inc(gelu_done, 1)
            act.wait_ge(cond_mm, 2)
            nc.scalar.activation(h2T[:], ps_y_flat[:, BANK:BANK + BATCH], ACT.Gelu,
                                 bias=small_sb[:, SMALL["b1"]]).then_inc(gelu_done, 1)
            act.wait_ge(att_step, 2)
            nc.scalar.activation(score_exp[:], score[:], ACT.Exp, bias=neg_max[:, 0:1],
                                 accum_out=exp_sum[:, 0:1]).then_inc(score_exped, 1)
            for n in range(3):
                split_weight(n)
            act.wait_ge(x_in[0], 16)
            x_high(0)
            for n in range(3, len(weights)):
                split_weight(n)
            act.wait_ge(mix_in[0], 16 * PAIR)
            mix_high(0)
            act.wait_ge(y_summed, 1)
            y_high(0, 0)
            act.wait_ge(y_summed, 2)
            y_high(0, 1)
            act.wait_ge(y_mm, HALVES)
            act.wait_ge(mix_in[1], 16 * PAIR)
            mix_high(1)
            act.wait_ge(x_in[1], 16)
            x_high(1)

            def tile(t, s, ahead, turn):
                if ahead >= 1:
                    act.wait_ge(y_summed, halves(t + 1, 0))
                    y_high((s + 1) % 2, 0)
                act.wait_ge(routed, t * ROUTE_STEPS + 3)
                nc.scalar.activation(ratio[:], top_gap[:], ACT.Exp).then_inc(ratio_done, 1)
                if ahead >= 2:
                    n, its_turn = (s + 2) % SLOTS, turn + (s + 2) // SLOTS
                    act.wait_ge(y_mm, halves(t + 1, 1))
                    act.wait_ge(mix_in[n], moved(its_turn, PAIR))
                    mix_high(n)
                    act.wait_ge(x_in[n], moved(its_turn))
                    x_high(n)
                if ahead >= 1:
                    act.wait_ge(y_summed, halves(t + 1, 1))
                    y_high((s + 1) % 2, 1)
                act.wait_ge(hwT_mm, t + 1)
                nc.scalar.copy(hwT_hi[:], ps_main[:, 1 - s % 2, 0, 0:P]).then_inc(hwT_hi_done, 1)

            over_tiles(act, tile)

        @block.gpsimd
        def _(pool):
            nc.gpsimd.memset(mix[:], 0.0).then_inc(mix_zeroed, 1)

            def mix_low(s):
                nc.gpsimd.tensor_tensor(mix_parts[:, P:2 * P], mix[:, s, :], mix_parts[:, 0:P].bitcast(F32),
                                        ALU.subtract).then_inc(mix_lo_done, 1)

            def add_bias(s):
                nc.gpsimd.tensor_tensor(x_sb[:, s, :], x_sb[:, s, :], bias_out[:], ALU.add).then_inc(x_biased, 1)

            for n in range(1, len(weights), 2):
                pool.wait_ge(w_hi_done, n + 1)
                nc.gpsimd.tensor_tensor(weights[n][2], staged(n), weights[n][1].bitcast(F32),
                                        ALU.subtract).then_inc(w_lo_done[1], 1)
            pool.wait_ge(mix_hi_done, 1)
            mix_low(0)
            pool.wait_ge(mix_hi_done, 2)
            mix_low(1)
            pool.wait_ge(bias_out_in, 16)
            pool.wait_ge(x_lo_done, 1)
            add_bias(0)

            def tile(t, s, ahead, turn):
                if ahead >= 1:
                    pool.wait_ge(x_lo_done, t + 2)
                    add_bias((s + 1) % SLOTS)
                if ahead >= 2:
                    pool.wait_ge(mix_hi_done, t + 3)
                    mix_low((s + 2) % SLOTS)

            over_tiles(pool, tile)

        @block.vector
        def _(dve):
            def split_weight(n):
                dve.wait_ge(w_hi_done, n + 1)
                nc.vector.tensor_tensor(weights[n][2], staged(n), weights[n][1].bitcast(F32),
                                        ALU.subtract).then_inc(w_lo_done[0], 1)

            def x_low(s):
                nc.vector.tensor_tensor(x_lo[:], x_sb[:, s, :], x_hi[:].bitcast(F32),
                                        ALU.subtract).then_inc(x_lo_done, 1)

            def y_sum(t, s, g):
                half = y_sb[:, g * HD:(g + 1) * HD].rearrange("p (c n) -> p c n", c=HC)
                dve.wait_ge(y_mm, halves(t, g))
                nc.vector.tensor_tensor(half, ps_y[:, :, 0, :],
                                        bias_y[:, s, :].unsqueeze(1).to_broadcast([P, HC, P]),
                                        ALU.add).then_inc(y_part, 1)
                dve.wait_ge(y_part, halves(t, g))
                nc.vector.tensor_tensor(half, ps_y[:, :, 1, :], half, ALU.add).then_inc(y_summed, 1)

            def y_low(t, u, g):
                half = slice(g * HD, (g + 1) * HD)
                dve.wait_ge(y_hi_done, halves(t, g))
                nc.vector.tensor_tensor(y_lo[:, u, half], y_sb[:, half], y_hi[:, u, half].bitcast(F32),
                                        ALU.subtract).then_inc(y_lo_done, 1)

            dve.wait_ge(cond_mm, 3)
            nc.vector.tensor_tensor(score[:], ps_y_flat[:, 0:KERNELS], small_sb[:, SMALL["b2"]],
                                    ALU.add).then_inc(att_step, 1)
            dve.wait_ge(att_step, 1)
            nc.vector.tensor_reduce(neg_max[:], score[:], AX_X, ALU.max, negate=True).then_inc(att_step, 1)
            dve.wait_ge(score_exped, 1)
            nc.vector.reciprocal(exp_inv[:], exp_sum[:]).then_inc(att_step, 1)
            dve.wait_ge(att_step, 3)
            nc.vector.tensor_scalar(att[:], score_exp[:], exp_inv[:, 0:1], None, ALU.mult).then_inc(att_step, 1)
            dve.wait_ge(cond_mm, 4)
            nc.vector.tensor_copy(attT[:], ps_y_flat[0:KERNELS, BANK:BANK + BATCH]).then_inc(att_step, 1)
            dve.wait_ge(agg_b_mm, 1)
            nc.vector.tensor_copy(agg_b[:], ps_y_flat[:, 0:CH]).then_inc(agg_b_done, 1)
            low = list(range(0, len(weights), 2))
            for g in range(CH * CH // BANK):
                if g % 2 == 0:
                    split_weight(low.pop(0))
                if g == 5:
                    dve.wait_ge(x_hi_done, 1)
                    x_low(0)
                dve.wait_ge(agg_mm, g + 1)
                nc.vector.tensor_copy(agg_w[:, g * BANK:(g + 1) * BANK],
                                      ps_main[:, g // 3 % 2, g % 3, :]).then_inc(agg_done, 1)
            while low:
                split_weight(low.pop(0))
            dve.wait_ge(bias_y_in[0], 16)
            for g in range(HALVES):
                y_sum(0, 0, g)
                y_low(0, 0, g)
            dve.wait_ge(x_hi_done, 2)
            x_low(1)

            def tile(t, s, ahead, turn):
                u = s % 2
                after = (s + 1) % SLOTS
                if ahead >= 1:
                    dve.wait_ge(bias_y_in[after], moved(turn + (s + 1) // SLOTS))
                    y_sum(t + 1, after, 0)
                    y_low(t + 1, 1 - u, 0)
                step = t * ROUTE_STEPS
                logits = ps_main[:, u, 0, ER:AR]
                dve.wait_ge(ar_mm, t + 1)
                nc.vector.tensor_copy(logits_sb[:], logits).then_inc(routed, 1)
                nc.vector.max(top_val[:], logits).then_inc(routed, 1)
                dve.wait_ge(routed, step + 2)
                nc.vector.tensor_tensor(top_gap[:], top_val[:, 1:2], top_val[:, 0:1],
                                        ALU.subtract).then_inc(routed, 1)
                nc.vector.max_index(top_idx[:], top_val[:], logits_sb[:]).then_inc(routed, 1)
                dve.wait_ge(routed, step + 4)
                nc.vector.tensor_tensor(picked[:], expert_no,
                                        top_idx[:, 0:2].unsqueeze(2).to_broadcast([P, 2, EXPERTS]),
                                        ALU.is_equal).then_inc(routed, 1)
                dve.wait_ge(ratio_done, t + 1)
                nc.vector.tensor_scalar(scaled_sum[:], ratio[:], 1.0 / LORA_SCALE, 1.0 / LORA_SCALE,
                                        ALU.mult, ALU.add).then_inc(routed, 1)
                dve.wait_ge(routed, step + 5)
                nc.vector.scalar_tensor_tensor(expert_w[:], picked[:, 1, :], ratio[:, 0:1], picked[:, 0, :],
                                               ALU.mult, ALU.add).then_inc(routed, 1)
                dve.wait_ge(routed, step + 6)
                nc.vector.reciprocal(first_w[:], scaled_sum[:]).then_inc(routed, 1)
                dve.wait_ge(routed, step + 8)
                nc.vector.scalar_tensor_tensor(
                    hw[:].rearrange("p (e r) -> p e r", e=EXPERTS),
                    ps_main[:, u, 0, 0:ER].rearrange("p (e r) -> p e r", e=EXPERTS), first_w[:, 0:1],
                    expert_w[:].unsqueeze(2).to_broadcast([P, EXPERTS, RANK]), ALU.mult, ALU.mult).then_inc(hw_done, 1)
                if ahead >= 1:
                    y_sum(t + 1, after, 1)
                    y_low(t + 1, 1 - u, 1)
                if ahead >= 2:
                    dve.wait_ge(x_hi_done, t + 3)
                    x_low((s + 2) % SLOTS)
                dve.wait_ge(hwT_hi_done, t + 1)
                nc.vector.tensor_tensor(hwT_lo[:], ps_main[:, 1 - u, 0, 0:P], hwT_hi[:].bitcast(F32),
                                        ALU.subtract).then_inc(hwT_lo_done, 1)
                res, at = out_columns(0)
                dve.wait_ge(x_biased, t + 1)
                dve.wait_ge(out_mm, t + 1)
                nc.vector.tensor_tensor(x_sb[:, s, res], ps_main[:, u, 0, at], x_sb[:, s, res], ALU.add)
                rest = x_sb[:, s, res.stop:D].rearrange("p (k n) -> p k n", k=2)
                nc.vector.tensor_tensor(rest, ps_main[:, u, 1:3, out_columns(1)[1]], rest,
                                        ALU.add).then_inc(out_done, 1)

            over_tiles(dve, tile)


def kernel(x, cond_128, L0_cond_W0, L0_cond_b0, L0_cond_W1, L0_cond_b1, L0_cond_W2, L0_cond_b2,
           L0_cond_weight, L0_cond_bias_k, L0_ffn_W_base, L0_ffn_b_base, L0_ffn_W_router, L0_ffn_A, L0_ffn_B):
    import concourse.bacc as bacc
    from concourse.bass_utils import run_bass_kernel_spmd

    def lay(a):
        return np.ascontiguousarray(a)

    x = np.asarray(x)
    small = np.zeros((P, SMALL_COLS), x.dtype)
    small[:, SMALL["condT"]] = np.asarray(cond_128).T
    small[:, SMALL["w0"]] = L0_cond_W0
    small[:, SMALL["b0"]] = np.asarray(L0_cond_b0).reshape(HID, 1)
    small[:, SMALL["w1"]] = L0_cond_W1
    small[:, SMALL["b1"]] = np.asarray(L0_cond_b1).reshape(HID, 1)
    small[:, SMALL["w2"]] = L0_cond_W2
    small[:, SMALL["b2"]] = np.asarray(L0_cond_b2).reshape(1, KERNELS)
    small[0:KERNELS, SMALL["mix_b"]] = L0_cond_bias_k
    small[:, SMALL["ident"]] = np.eye(P)
    small[:, SMALL["expert_no"]] = np.tile(np.arange(EXPERTS), 2)
    wide = np.concatenate([np.asarray(L0_ffn_A).reshape(ER, D), np.asarray(L0_ffn_W_router),
                           np.asarray(L0_ffn_W_base)], axis=0)
    arrays = {
        "x": lay(x.reshape(BATCH * CH, D)),
        "small": small,
        "mix_w": lay(np.asarray(L0_cond_weight)[..., 0].transpose(0, 2, 1).reshape(KERNELS, CH * CH)),
        "wide": lay(wide.T),
        "b_base": lay(L0_ffn_b_base),
        "bT": lay(np.asarray(L0_ffn_B).transpose(0, 2, 1).reshape(ER, D)),
    }
    nc = bacc.Bacc("TRN2", target_bir_lowering=False, num_devices=1)
    ins = [nc.dram_tensor("in_" + name, a.shape, mybir.dt.from_np(a.dtype), kind="ExternalInput").ap()
           for name, a in arrays.items()]
    out = nc.dram_tensor("result", (BATCH * CH, D), F32, kind="ExternalOutput").ap()
    build(nc, *ins, out)
    run = run_bass_kernel_spmd(nc, [{"in_" + name: a for name, a in arrays.items()}], core_ids=[0])
    return run.results[0]["result"].reshape(x.shape)
```

```python
from contextlib import ExitStack

import numpy as np

import concourse.bass as bass
from concourse import mybir

ALU = mybir.AluOpType
ACT = mybir.ActivationFunctionType
F32 = mybir.dt.float32
F32R = mybir.dt.float32r
U32 = mybir.dt.uint32
AX_X = mybir.AxisListType.X

P = 128
BATCH, CH, D = 128, 64, 1024
HID = 128
KERNELS = 8
EXPERTS, RANK = 8, 16
ER = EXPERTS * RANK
PAIR = P // CH
TILES = BATCH // PAIR
DC = D // P
BANK = 512
AR = ER + EXPERTS
WIDE = AR + D
CUTS = (0, 384, 772, WIDE)
SLOTS = 4
STAGE = 4
STAGE_CHUNKS = 4
LORA_SCALE = 2.0
HALVES = 2
HC = DC // HALVES
HD = D // HALVES

SMALL = {}
_at = 0
for _name, _width in (("condT", BATCH), ("w0", HID), ("b0", 1), ("w1", HID), ("b1", 1), ("w2", KERNELS),
                      ("b2", KERNELS), ("ident", P), ("expert_no", 2 * EXPERTS)):
    SMALL[_name] = slice(_at, _at + _width)
    _at += _width
SMALL_COLS = _at
MIX_COLS = CH + CH * CH
MIX_ROWS, ATT_LO = 40, slice(32, 40)


def out_columns(piece):
    first = max(CUTS[piece], AR)
    return slice(first - AR, CUTS[piece + 1] - AR), slice(first - CUTS[piece], CUTS[piece + 1] - CUTS[piece])


def build(nc, x, small, mix_w, wide, b_base, bT, out):
    x_tiles = x.rearrange("(t p) h -> t p h", p=P)
    out_tiles = out.rearrange("(t p) h -> t p h", p=P)
    agg_w_dram = nc.dram_tensor("agg_w_rows", (BATCH * CH, CH), F32, kind="Internal").ap()
    agg_b_dram = nc.dram_tensor("agg_b_rows", (BATCH * CH,), F32, kind="Internal").ap()
    agg_w_pairs = agg_w_dram.rearrange("(t p) o -> t p o", p=P)
    agg_b_pairs = agg_b_dram.rearrange("(t n) -> t n", n=P)

    with ExitStack() as ctx:
        def sb(name, shape, dt=F32):
            return ctx.enter_context(nc.sbuf_tensor(name, shape, dt))

        def sem(name):
            return ctx.enter_context(nc.semaphore(name))

        w_hi = sb("w_hi", [P, DC, WIDE], F32R)
        w_lo = sb("w_lo", [P, DC, WIDE], F32R)
        b_hi = sb("b_hi", [P, D], F32R)
        b_lo = sb("b_lo", [P, D], F32R)
        bias_out = sb("bias_out", [P, D])
        x_sb = sb("x_sb", [P, SLOTS, D])
        x_hi = sb("x_hi", [P, 2, D], F32R)
        x_lo = sb("x_lo", [P, 2, D], F32R)
        mix = sb("mix", [P, SLOTS, P])
        mix_parts = sb("mix_parts", [P, 2, 2 * P], F32R)
        bias_y = sb("bias_y", [P, SLOTS, P])
        y_sb = sb("y_sb", [P, D])
        y_parts = sb("y_parts", [P, 2 * 2 * D + CH], F32R)
        y_hi = y_parts[:, 0:2 * D].rearrange("p (u n) -> p u n", u=2)
        y_lo = y_parts[:, 2 * D:4 * D].rearrange("p (u n) -> p u n", u=2)
        mix_w_parts = y_parts[0:MIX_ROWS, 0:MIX_COLS]
        logits_sb = sb("logits_sb", [P, EXPERTS])
        top_val = sb("top_val", [P, 8])
        top_gap = sb("top_gap", [P, 1])
        top_idx = sb("top_idx", [P, 8], U32)
        picked = sb("picked", [P, 2, EXPERTS])
        ratio = sb("ratio", [P, 1])
        scaled_sum = sb("scaled_sum", [P, 1])
        first_w = sb("first_w", [P, 1])
        expert_w = sb("expert_w", [P, EXPERTS])
        hw = sb("hw", [P, ER])
        hwT_hi = sb("hwT_hi", [P, P], F32R)
        hwT_lo = sb("hwT_lo", [P, P], F32R)
        small_sb = sb("small_sb", [P, SMALL_COLS])
        w_stage = sb("w_stage", [P, STAGE, STAGE_CHUNKS * (CUTS[3] - CUTS[2])])
        h1T = sb("h1T", [P, BATCH])
        h2T = sb("h2T", [P, BATCH])
        score = sb("score", [P, KERNELS])
        neg_max = sb("neg_max", [P, 1])
        score_exp = sb("score_exp", [P, KERNELS])
        exp_sum = sb("exp_sum", [P, 1])
        exp_inv = sb("exp_inv", [P, 1])
        att = sb("att", [P, MIX_ROWS])
        attT = sb("attT", [MIX_ROWS, BATCH], F32R)
        mix_space = sb("mix_space", [BATCH, MIX_COLS])
        mix_w_raw = mix_space[0:MIX_ROWS, :]
        agg_w = mix_space[:, 0:CH * CH]
        agg_b = sb("agg_b", [BATCH, CH])

        ident = small_sb[:, SMALL["ident"]]
        expert_no = small_sb[:, SMALL["expert_no"]].rearrange("p (s e) -> p s e", s=2)

        ps_main = ctx.enter_context(nc.psum_tensor("ps_main", [P, 2, 3, BANK], F32))
        ps_y = ctx.enter_context(nc.psum_tensor("ps_y", [P, HC, 2, P], F32))
        ps_y_flat = ps_y[:].rearrange("p c k n -> p (c k n)")
        ps_y_first = ps_main[:, 1, 1:3, :].rearrange("p h (c k n) -> p (h c) k n", k=2, n=P)

        small_in = sem("small_in")
        mix_w_in = sem("mix_w_in")
        w_in = [sem(f"w_in{s}") for s in range(STAGE)]
        bias_out_in = sem("bias_out_in")
        cond_mm = sem("cond_mm")
        gelu_done = sem("gelu_done")
        att_step = sem("att_step")
        score_exped = sem("score_exped")
        mix_w_hi_done = [sem("mix_w_hi_done_dve"), sem("mix_w_hi_done_act")]
        mix_w_lo_done = [sem("mix_w_lo_done_dve"), sem("mix_w_lo_done_pool")]
        attT_hi_done = sem("attT_hi_done")
        attT_lo_done = sem("attT_lo_done")
        agg_b_mm = sem("agg_b_mm")
        agg_b_done = sem("agg_b_done")
        agg_mm = sem("agg_mm")
        agg_done = [sem("agg_done_dve"), sem("agg_done_act")]
        agg_b_out = sem("agg_b_out")
        agg_w_out = sem("agg_w_out")
        mix_zeroed = sem("mix_zeroed")
        w_hi_done = sem("w_hi_done")
        w_lo_done = [sem("w_lo_done_dve"), sem("w_lo_done_pool")]
        x_in = [sem(f"x_in{s}") for s in range(SLOTS)]
        mix_in = [sem(f"mix_in{s}") for s in range(SLOTS)]
        bias_y_in = [sem(f"bias_y_in{s}") for s in range(SLOTS)]
        stored = [sem(f"stored{s}") for s in range(SLOTS)]
        x_hi_done = sem("x_hi_done")
        x_lo_done = sem("x_lo_done")
        x_biased = sem("x_biased")
        mix_hi_done = sem("mix_hi_done")
        mix_lo_done = sem("mix_lo_done")
        y_mm = sem("y_mm")
        y_part = sem("y_part")
        y_summed = sem("y_summed")
        y_hi_done = sem("y_hi_done")
        y_lo_done = sem("y_lo_done")
        ar_mm = sem("ar_mm")
        routed = sem("routed")
        ratio_done = sem("ratio_done")
        hw_done = sem("hw_done")
        hwT_mm = sem("hwT_mm")
        hwT_hi_done = sem("hwT_hi_done")
        hwT_lo_done = sem("hwT_lo_done")
        out_mm = sem("out_mm")
        out_done = sem("out_done")
        ROUTE_STEPS = 8
        AGG_BANKS = CH * CH // BANK
        QUARTER = MIX_COLS // 4

        wide_chunks = wide.rearrange("(c p) n -> p c n", p=P)
        weights = []
        for k in range(3):
            piece, width = slice(CUTS[k], CUTS[k + 1]), CUTS[k + 1] - CUTS[k]
            for c in range(0, DC, STAGE_CHUNKS):
                part = (slice(None), slice(c, c + STAGE_CHUNKS), piece)
                stage = w_stage[:, len(weights) % STAGE, 0:STAGE_CHUNKS * width]
                weights.append((wide_chunks[part], stage.rearrange("p (c n) -> p c n", n=width),
                                w_hi[part], w_lo[part]))
        weights.append((bT, w_stage[:, len(weights) % STAGE, 0:D], b_hi[:], b_lo[:]))
        LOW_BY = [1, 0, 1, 0, 1, 1, 1]

        def weight_low_part(engine, n):
            _, stage, high, low = weights[n]
            return engine.tensor_tensor(low, stage, high.bitcast(F32), ALU.subtract)

        def wait_split(eng, n):
            eng.wait_ge(w_lo_done[LOW_BY[n]], LOW_BY[:n + 1].count(LOW_BY[n]))

        def over_tiles(eng, tile):
            with eng.Fori(0, TILES // SLOTS - 1) as turn:
                for s in range(SLOTS):
                    tile(turn * SLOTS + s, s, SLOTS, turn)
            for s in range(SLOTS):
                tile(TILES - SLOTS + s, s, SLOTS - 1 - s, TILES // SLOTS - 1)

        def mix_quarter(q):
            return slice(q * QUARTER, (q + 1) * QUARTER), q // 2, q % 2 + 1

        def mix_low_parts(engine, q):
            cols, low = mix_quarter(q)[0], slice(0, KERNELS)
            return engine.tensor_tensor(mix_w_parts[low, cols], mix_w_raw[low, cols],
                                        mix_w_parts[low, cols].bitcast(F32), ALU.subtract)

        def moved(turn, dmas=1):
            return turn * (16 * dmas) + 16 * dmas

        def halves(t, g):
            return t * HALVES + g + 1

        block = ctx.enter_context(nc.Block())

        @block.sync
        def _(sp):
            def load_mix(s, pair):
                for par in range(PAIR):
                    blk = slice(par * CH, (par + 1) * CH)
                    sp.dma_start(mix[blk, s, blk], pair[blk, :]).then_inc(mix_in[s], 16)

            def load_first_mix(t):
                for par in range(PAIR):
                    b, blk = t * PAIR + par, slice(par * CH, (par + 1) * CH)
                    sp.dma_start(mix[blk, t, blk], agg_w[b:b + 1, :].rearrange("b (i o) -> b i o", i=CH)
                                 ).then_inc(mix_in[t], 16)

            def load_bias_y(s, t):
                sp.dma_start(bias_y[:, s, :], agg_b_pairs[t].partition_broadcast(P)).then_inc(bias_y_in[s], 16)

            def load_x(t):
                sp.dma_start(x_sb[:, t, :], x_tiles[t]).then_inc(x_in[t], 16)

            def load_weight(n):
                if n >= STAGE:
                    wait_split(sp, n - STAGE)
                source, stage = weights[n][:2]
                sp.dma_start(stage, source).then_inc(w_in[n % STAGE], 16)

            sp.dma_start(small_sb[:], small).then_inc(small_in, 16)
            sp.dma_start(mix_w_raw, mix_w).then_inc(mix_w_in, 16)
            load_x(0)
            load_weight(0)
            load_x(1)
            sp.dma_start(bias_out[:], b_base.partition_broadcast(P)).then_inc(bias_out_in, 16)
            load_weight(1)
            sp.wait_ge(agg_b_done, 1)
            sp.dma_start(agg_b_dram.rearrange("(b o) -> b o", b=BATCH), agg_b[:]).then_inc(agg_b_out, 16)
            load_weight(2)
            sp.wait_ge(agg_b_out, 16)
            load_bias_y(0, 0)
            sp.wait_ge(mix_zeroed, 1)
            for n in range(2):
                sp.wait_ge(agg_done[n], AGG_BANKS // 2)
            load_first_mix(0)
            load_first_mix(1)
            load_bias_y(1, 1)
            for n in range(3, 6):
                load_weight(n)
            for t in range(2, SLOTS):
                load_x(t)
                load_bias_y(t, t)
                load_first_mix(t)
            load_weight(6)
            sp.dma_start(agg_w_dram.rearrange("(b i) o -> b (i o)", b=BATCH), agg_w).then_inc(agg_w_out, 16)
            sp.wait_ge(agg_w_out, 16)

            def tile(t, s, ahead, turn):
                sp.wait_ge(out_done, t + 1)
                sp.dma_start(out_tiles[t], x_sb[:, s, :]).then_inc(stored[s], 16)
                if ahead >= SLOTS:
                    load_mix(s, agg_w_pairs[t + SLOTS])
                    load_bias_y(s, t + SLOTS)
                    sp.wait_ge(stored[s], moved(turn))
                    sp.dma_start(x_sb[:, s, :], x_tiles[t + SLOTS]).then_inc(x_in[s], 16)

            over_tiles(sp, tile)
            for s in range(SLOTS):
                sp.wait_ge(stored[s], 16 * (TILES // SLOTS))

        @block.tensor
        def _(pe):
            def y_products(u, g, into=ps_y):
                for j in range(HC):
                    cols = slice((g * HC + j) * P, (g * HC + j + 1) * P)
                    dst = into[:, j, :, :].rearrange("p k n -> p (k n)")
                    nc.tensor.matmul(dst, x_hi[:, u, cols], mix_parts[:, u, :], start=True, stop=False)
                    mm = nc.tensor.matmul(dst, x_lo[:, u, cols], mix_parts[:, u, :], start=False, stop=True)
                mm.then_inc(y_mm, 1)

            def piece_products(u, k, c):
                cols, piece = slice(c * P, (c + 1) * P), slice(CUTS[k], CUTS[k + 1])
                dst = ps_main[:, u, k, 0:CUTS[k + 1] - CUTS[k]]
                nc.tensor.matmul(dst, y_hi[:, u, cols], w_hi[:, c, piece], start=c == 0, stop=False)
                nc.tensor.matmul(dst, y_hi[:, u, cols], w_lo[:, c, piece], start=False, stop=False)
                return nc.tensor.matmul(dst, y_lo[:, u, cols], w_hi[:, c, piece], start=False, stop=c == DC - 1)

            def expert_products(u, stat, mov):
                for k in range(3):
                    res, at = out_columns(k)
                    mm = nc.tensor.matmul(ps_main[:, u, k, at], stat[:], mov[:, res], start=False, stop=True,
                                          skip_group_check=True)
                return mm

            def chain(dst, stat, mov, done):
                nc.tensor.matmul(dst, stat, mov, start=True, stop=True).then_inc(done, 1)

            pe.wait_ge(small_in, 16)
            chain(ps_y_flat[:, 0:BATCH], small_sb[:, SMALL["w0"]], small_sb[:, SMALL["condT"]], cond_mm)
            pe.wait_ge(gelu_done, 1)
            chain(ps_y_flat[:, BANK:BANK + BATCH], small_sb[:, SMALL["w1"]], h1T[:], cond_mm)
            pe.wait_ge(gelu_done, 2)
            chain(ps_y_flat[:, 0:KERNELS], h2T[:], small_sb[:, SMALL["w2"]], cond_mm)
            pe.wait_ge(att_step, 4)
            chain(ps_y_flat[0:MIX_ROWS, BANK:BANK + BATCH], att[:], ident, cond_mm)
            pe.wait_ge(attT_lo_done, 1)

            pe.wait_ge(mix_w_lo_done[0], 1)
            chain(ps_y_flat[:, 0:CH], attT[:], mix_w_parts[:, 0:CH], agg_b_mm)
            for g in range(AGG_BANKS):
                cols = slice(CH + g * BANK, CH + (g + 1) * BANK)
                _, maker, count = mix_quarter(-(-cols.stop // QUARTER) - 1)
                pe.wait_ge(mix_w_lo_done[maker], count)
                if g >= 6:
                    pe.wait_ge(agg_done[g % 2], (g - 6) // 2 + 1)
                chain(ps_main[:, g // 3 % 2, g % 3, :], attT[:], mix_w_parts[:, cols], agg_mm)

            pe.wait_ge(agg_b_done, 1)
            pe.wait_ge(x_lo_done, 1)
            pe.wait_ge(mix_lo_done, 1)
            y_products(0, 0)
            for n in range(2):
                pe.wait_ge(agg_done[n], AGG_BANKS // 2)
            y_products(0, 1, into=ps_y_first)

            def tile(t, s, ahead, turn):
                u = s % 2
                if ahead >= 1:
                    pe.wait_ge(x_lo_done, t + 2)
                    pe.wait_ge(mix_lo_done, t + 2)
                    pe.wait_ge(y_summed, halves(t, 1))
                    y_products(1 - u, 0)
                for c in range(DC):
                    if c % HC == 0:
                        pe.wait_ge(y_lo_done, halves(t, c // HC))
                        wait_split(pe, c // HC)
                    mm = piece_products(u, 0, c)
                mm.then_inc(ar_mm, 1)
                if ahead >= 1:
                    pe.wait_ge(y_summed, halves(t + 1, 0))
                    y_products(1 - u, 1)
                for c in range(DC):
                    if c % HC == 0:
                        wait_split(pe, 2 + c // HC)
                    piece_products(u, 1, c)
                for c in range(DC):
                    if c % HC == 0:
                        wait_split(pe, 4 + c // HC)
                    if c == DC - 2:
                        pe.wait_ge(hw_done, t + 1)
                        nc.tensor.transpose(ps_main[:, 1 - u, 0, 0:P], hw[:], ident).then_inc(hwT_mm, 1)
                    piece_products(u, 2, c)
                wait_split(pe, 6)
                pe.wait_ge(hwT_hi_done, t + 1)
                expert_products(u, hwT_hi, b_hi)
                expert_products(u, hwT_hi, b_lo)
                pe.wait_ge(hwT_lo_done, t + 1)
                expert_products(u, hwT_lo, b_hi).then_inc(out_mm, 1)

            over_tiles(pe, tile)

        @block.scalar
        def _(act):
            def split_weight(n):
                act.wait_ge(w_in[n % STAGE], 16 * (n // STAGE + 1))
                _, stage, high, _ = weights[n]
                nc.scalar.copy(high, stage).then_inc(w_hi_done, 1)

            def x_high(s):
                nc.scalar.copy(x_hi[:, s % 2, :], x_sb[:, s, :]).then_inc(x_hi_done, 1)

            def mix_high(s):
                nc.scalar.copy(mix_parts[:, s % 2, 0:P], mix[:, s, :]).then_inc(mix_hi_done, 1)

            def y_high(u, g):
                half = slice(g * HD, (g + 1) * HD)
                nc.scalar.copy(y_hi[:, u, half], y_sb[:, half]).then_inc(y_hi_done, 1)

            def mix_w_high(q):
                cols = mix_quarter(q)[0]
                nc.scalar.copy(mix_w_parts[:, cols], mix_w_raw[:, cols]).then_inc(mix_w_hi_done[1], 1)

            act.wait_ge(cond_mm, 1)
            nc.scalar.activation(h1T[:], ps_y_flat[:, 0:BATCH], ACT.Gelu,
                                 bias=small_sb[:, SMALL["b0"]]).then_inc(gelu_done, 1)
            act.wait_ge(cond_mm, 2)
            nc.scalar.activation(h2T[:], ps_y_flat[:, BANK:BANK + BATCH], ACT.Gelu,
                                 bias=small_sb[:, SMALL["b1"]]).then_inc(gelu_done, 1)
            act.wait_ge(mix_w_in, 16)
            mix_w_high(2)
            act.wait_ge(att_step, 2)
            nc.scalar.activation(score_exp[:], score[:], ACT.Exp, bias=neg_max[:, 0:1],
                                 accum_out=exp_sum[:, 0:1]).then_inc(score_exped, 1)
            mix_w_high(3)
            act.wait_ge(cond_mm, 4)
            nc.scalar.copy(attT[:], ps_y_flat[0:MIX_ROWS, BANK:BANK + BATCH]).then_inc(attT_hi_done, 1)
            act.wait_ge(x_in[0], 16)
            x_high(0)
            for g in range(1, AGG_BANKS, 2):
                act.wait_ge(agg_mm, g + 1)
                nc.scalar.copy(agg_w[:, g * BANK:(g + 1) * BANK],
                               ps_main[:, g // 3 % 2, g % 3, :]).then_inc(agg_done[1], 1)
            split_weight(0)
            split_weight(1)
            act.wait_ge(mix_in[0], 16 * PAIR)
            mix_high(0)
            act.wait_ge(x_in[1], 16)
            x_high(1)
            act.wait_ge(mix_in[1], 16 * PAIR)
            mix_high(1)
            split_weight(2)
            split_weight(3)
            for g in range(HALVES):
                act.wait_ge(y_summed, g + 1)
                y_high(0, g)
            for n in range(4, len(weights)):
                split_weight(n)

            def tile(t, s, ahead, turn):
                if ahead >= 1:
                    act.wait_ge(y_summed, halves(t + 1, 0))
                    y_high((s + 1) % 2, 0)
                act.wait_ge(routed, t * ROUTE_STEPS + 3)
                nc.scalar.activation(ratio[:], top_gap[:], ACT.Exp).then_inc(ratio_done, 1)
                if ahead >= 2:
                    n, its_turn = (s + 2) % SLOTS, turn + (s + 2) // SLOTS
                    act.wait_ge(y_mm, halves(t, 1))
                    act.wait_ge(mix_in[n], moved(its_turn, PAIR))
                    mix_high(n)
                    act.wait_ge(x_in[n], moved(its_turn))
                    x_high(n)
                if ahead >= 1:
                    act.wait_ge(y_summed, halves(t + 1, 1))
                    y_high((s + 1) % 2, 1)
                act.wait_ge(hwT_mm, t + 1)
                nc.scalar.copy(hwT_hi[:], ps_main[:, 1 - s % 2, 0, 0:P]).then_inc(hwT_hi_done, 1)

            over_tiles(act, tile)

        @block.gpsimd
        def _(pool):
            nc.gpsimd.memset(mix[:], 0.0).then_inc(mix_zeroed, 1)

            def mix_low(s):
                u = s % 2
                nc.gpsimd.tensor_tensor(mix_parts[:, u, P:2 * P], mix[:, s, :], mix_parts[:, u, 0:P].bitcast(F32),
                                        ALU.subtract).then_inc(mix_lo_done, 1)

            def add_bias(s):
                nc.gpsimd.tensor_tensor(x_sb[:, s, :], x_sb[:, s, :], bias_out[:], ALU.add).then_inc(x_biased, 1)

            def split_weight(n):
                pool.wait_ge(w_hi_done, n + 1)
                weight_low_part(nc.gpsimd, n).then_inc(w_lo_done[1], 1)

            pool.wait_ge(mix_zeroed, 1)
            for q in range(2, 4):
                _, maker, count = mix_quarter(q)
                pool.wait_ge(mix_w_hi_done[maker], count)
                mix_low_parts(nc.gpsimd, q).then_inc(mix_w_lo_done[maker], 1)
            pool.wait_ge(mix_w_lo_done[1], 2)
            pool.wait_ge(bias_out_in, 16)
            pool.wait_ge(x_lo_done, 1)
            add_bias(0)
            for n in range(len(weights)):
                if LOW_BY[n] == 1:
                    split_weight(n)

            def tile(t, s, ahead, turn):
                if ahead >= 1:
                    pool.wait_ge(x_lo_done, t + 2)
                    add_bias((s + 1) % SLOTS)
                if ahead >= 2:
                    pool.wait_ge(mix_hi_done, t + 3)
                    mix_low((s + 2) % SLOTS)

            over_tiles(pool, tile)

        @block.vector
        def _(dve):
            def split_weight(n):
                dve.wait_ge(w_hi_done, n + 1)
                weight_low_part(nc.vector, n).then_inc(w_lo_done[0], 1)

            def x_low(s):
                u = s % 2
                nc.vector.tensor_tensor(x_lo[:, u, :], x_sb[:, s, :], x_hi[:, u, :].bitcast(F32),
                                        ALU.subtract).then_inc(x_lo_done, 1)

            def mix_low(s):
                dve.wait_ge(mix_hi_done, s + 1)
                nc.vector.tensor_tensor(mix_parts[:, s, P:2 * P], mix[:, s, :], mix_parts[:, s, 0:P].bitcast(F32),
                                        ALU.subtract).then_inc(mix_lo_done, 1)

            def y_sum(t, s, g, from_=ps_y):
                half = y_sb[:, g * HD:(g + 1) * HD].rearrange("p (c n) -> p c n", c=HC)
                dve.wait_ge(y_mm, halves(t, g))
                nc.vector.tensor_tensor(half, from_[:, :, 0, :],
                                        bias_y[:, s, :].unsqueeze(1).to_broadcast([P, HC, P]),
                                        ALU.add).then_inc(y_part, 1)
                dve.wait_ge(y_part, halves(t, g))
                nc.vector.tensor_tensor(half, from_[:, :, 1, :], half, ALU.add).then_inc(y_summed, 1)

            def y_low(t, u, g):
                half = slice(g * HD, (g + 1) * HD)
                dve.wait_ge(y_hi_done, halves(t, g))
                nc.vector.tensor_tensor(y_lo[:, u, half], y_sb[:, half], y_hi[:, u, half].bitcast(F32),
                                        ALU.subtract).then_inc(y_lo_done, 1)

            def mix_w_high(q):
                cols, maker, count = mix_quarter(q)
                nc.vector.tensor_copy(mix_w_parts[:, cols], mix_w_raw[:, cols]).then_inc(mix_w_hi_done[maker], 1)

            def mix_w_low(q):
                _, maker, count = mix_quarter(q)
                dve.wait_ge(mix_w_hi_done[maker], count)
                mix_low_parts(nc.vector, q).then_inc(mix_w_lo_done[maker], 1)

            dve.wait_ge(mix_w_in, 16)
            mix_w_high(0)
            mix_w_low(0)
            dve.wait_ge(cond_mm, 3)
            nc.vector.tensor_tensor(score[:], ps_y_flat[:, 0:KERNELS], small_sb[:, SMALL["b2"]],
                                    ALU.add).then_inc(att_step, 1)
            dve.wait_ge(att_step, 1)
            nc.vector.tensor_reduce(neg_max[:], score[:], AX_X, ALU.max, negate=True).then_inc(att_step, 1)
            mix_w_high(1)
            dve.wait_ge(score_exped, 1)
            nc.vector.reciprocal(exp_inv[:], exp_sum[:]).then_inc(att_step, 1)
            dve.wait_ge(att_step, 3)
            blocks = MIX_ROWS // KERNELS
            nc.vector.tensor_scalar(att[:].rearrange("p (r k) -> p r k", r=blocks),
                                    score_exp[:].unsqueeze(1).to_broadcast([P, blocks, KERNELS]),
                                    exp_inv[:, 0:1], None, ALU.mult).then_inc(att_step, 1)
            mix_w_low(1)
            dve.wait_ge(attT_hi_done, 1)
            nc.vector.tensor_tensor(attT[ATT_LO, :], ps_y_flat[ATT_LO, BANK:BANK + BATCH],
                                    attT[ATT_LO, :].bitcast(F32), ALU.subtract).then_inc(attT_lo_done, 1)
            dve.wait_ge(agg_b_mm, 1)
            nc.vector.tensor_copy(agg_b[:], ps_y_flat[:, 0:CH]).then_inc(agg_b_done, 1)
            dve.wait_ge(x_hi_done, 1)
            x_low(0)
            for g in range(0, AGG_BANKS, 2):
                dve.wait_ge(agg_mm, g + 1)
                nc.vector.tensor_copy(agg_w[:, g * BANK:(g + 1) * BANK],
                                      ps_main[:, g // 3 % 2, g % 3, :]).then_inc(agg_done[0], 1)
            mix_low(0)
            split_weight(1)
            dve.wait_ge(x_hi_done, 2)
            x_low(1)
            mix_low(1)
            dve.wait_ge(bias_y_in[0], 16)
            y_sum(0, 0, 0)
            y_sum(0, 0, 1, from_=ps_y_first)
            y_low(0, 0, 0)
            y_low(0, 0, 1)
            split_weight(3)
            dve.wait_ge(y_lo_done, HALVES)

            def tile(t, s, ahead, turn):
                u = s % 2
                after = (s + 1) % SLOTS
                if ahead >= 1:
                    dve.wait_ge(bias_y_in[after], moved(turn + (s + 1) // SLOTS))
                    y_sum(t + 1, after, 0)
                    y_low(t + 1, 1 - u, 0)
                step = t * ROUTE_STEPS
                logits = ps_main[:, u, 0, ER:AR]
                dve.wait_ge(ar_mm, t + 1)
                nc.vector.tensor_copy(logits_sb[:], logits).then_inc(routed, 1)
                nc.vector.max(top_val[:], logits).then_inc(routed, 1)
                dve.wait_ge(routed, step + 2)
                nc.vector.tensor_tensor(top_gap[:], top_val[:, 1:2], top_val[:, 0:1],
                                        ALU.subtract).then_inc(routed, 1)
                nc.vector.max_index(top_idx[:], top_val[:], logits_sb[:]).then_inc(routed, 1)
                dve.wait_ge(routed, step + 4)
                nc.vector.tensor_tensor(picked[:], expert_no,
                                        top_idx[:, 0:2].unsqueeze(2).to_broadcast([P, 2, EXPERTS]),
                                        ALU.is_equal).then_inc(routed, 1)
                dve.wait_ge(ratio_done, t + 1)
                nc.vector.tensor_scalar(scaled_sum[:], ratio[:], 1.0 / LORA_SCALE, 1.0 / LORA_SCALE,
                                        ALU.mult, ALU.add).then_inc(routed, 1)
                dve.wait_ge(routed, step + 5)
                nc.vector.scalar_tensor_tensor(expert_w[:], picked[:, 1, :], ratio[:, 0:1], picked[:, 0, :],
                                               ALU.mult, ALU.add).then_inc(routed, 1)
                dve.wait_ge(routed, step + 6)
                nc.vector.reciprocal(first_w[:], scaled_sum[:]).then_inc(routed, 1)
                dve.wait_ge(routed, step + 8)
                nc.vector.scalar_tensor_tensor(
                    hw[:].rearrange("p (e r) -> p e r", e=EXPERTS),
                    ps_main[:, u, 0, 0:ER].rearrange("p (e r) -> p e r", e=EXPERTS), first_w[:, 0:1],
                    expert_w[:].unsqueeze(2).to_broadcast([P, EXPERTS, RANK]), ALU.mult, ALU.mult).then_inc(hw_done, 1)
                if ahead >= 1:
                    y_sum(t + 1, after, 1)
                    y_low(t + 1, 1 - u, 1)
                if ahead >= 2:
                    dve.wait_ge(x_hi_done, t + 3)
                    x_low((s + 2) % SLOTS)
                dve.wait_ge(hwT_hi_done, t + 1)
                nc.vector.tensor_tensor(hwT_lo[:], ps_main[:, 1 - u, 0, 0:P], hwT_hi[:].bitcast(F32),
                                        ALU.subtract).then_inc(hwT_lo_done, 1)
                res, at = out_columns(0)
                dve.wait_ge(x_biased, t + 1)
                dve.wait_ge(out_mm, t + 1)
                nc.vector.tensor_tensor(x_sb[:, s, res], ps_main[:, u, 0, at], x_sb[:, s, res], ALU.add)
                rest = x_sb[:, s, res.stop:D].rearrange("p (k n) -> p k n", k=2)
                nc.vector.tensor_tensor(rest, ps_main[:, u, 1:3, out_columns(1)[1]], rest,
                                        ALU.add).then_inc(out_done, 1)

            over_tiles(dve, tile)


def kernel(x, cond_128, L0_cond_W0, L0_cond_b0, L0_cond_W1, L0_cond_b1, L0_cond_W2, L0_cond_b2,
           L0_cond_weight, L0_cond_bias_k, L0_ffn_W_base, L0_ffn_b_base, L0_ffn_W_router, L0_ffn_A, L0_ffn_B):
    import concourse.bacc as bacc
    from concourse.bass_utils import run_bass_kernel_spmd

    def lay(a):
        return np.ascontiguousarray(a)

    x = np.asarray(x)
    small = np.zeros((P, SMALL_COLS), x.dtype)
    small[:, SMALL["condT"]] = np.asarray(cond_128).T
    small[:, SMALL["w0"]] = L0_cond_W0
    small[:, SMALL["b0"]] = np.asarray(L0_cond_b0).reshape(HID, 1)
    small[:, SMALL["w1"]] = L0_cond_W1
    small[:, SMALL["b1"]] = np.asarray(L0_cond_b1).reshape(HID, 1)
    small[:, SMALL["w2"]] = L0_cond_W2
    small[:, SMALL["b2"]] = np.asarray(L0_cond_b2).reshape(1, KERNELS)
    small[:, SMALL["ident"]] = np.eye(P)
    small[:, SMALL["expert_no"]] = np.tile(np.arange(EXPERTS), 2)
    wide = np.concatenate([np.asarray(L0_ffn_A).reshape(ER, D), np.asarray(L0_ffn_W_router),
                           np.asarray(L0_ffn_W_base)], axis=0)
    mix_rows = np.concatenate([L0_cond_bias_k, np.asarray(L0_cond_weight)[..., 0].transpose(0, 2, 1)
                               .reshape(KERNELS, CH * CH)], axis=1)
    mix_w = np.zeros((MIX_ROWS, MIX_COLS), mix_rows.dtype)
    for first in (0, KERNELS, ATT_LO.start):
        mix_w[first:first + KERNELS] = mix_rows
    arrays = {
        "x": lay(x.reshape(BATCH * CH, D)),
        "small": small,
        "mix_w": mix_w,
        "wide": lay(wide.T),
        "b_base": lay(L0_ffn_b_base),
        "bT": lay(np.asarray(L0_ffn_B).transpose(0, 2, 1).reshape(ER, D)),
    }
    nc = bacc.Bacc("TRN2", target_bir_lowering=False, num_devices=1)
    ins = [nc.dram_tensor("in_" + name, a.shape, mybir.dt.from_np(a.dtype), kind="ExternalInput").ap()
           for name, a in arrays.items()]
    out = nc.dram_tensor("result", (BATCH * CH, D), F32, kind="ExternalOutput").ap()
    build(nc, *ins, out)
    run = run_bass_kernel_spmd(nc, [{"in_" + name: a for name, a in arrays.items()}], core_ids=[0])
    return run.results[0]["result"].reshape(x.shape)
```
